# Optimizing a Trainium2 kernel written in Bass

```python
import numpy as np
import jax
import jax.numpy as jnp

def _softmax(x, axis=-1):
    return jax.nn.softmax(x, axis=axis)

def _gelu(x):
    return jax.nn.gelu(x, approximate=True)

def _silu(x):
    return jax.nn.silu(x)

def _sigmoid(x):
    return jax.nn.sigmoid(x)

def _layernorm(x, axis=-1, eps=1e-05):
    m = jnp.mean(x, axis=axis, keepdims=True)
    v = jnp.var(x, axis=axis, keepdims=True)
    return (x - m) / jnp.sqrt(v + eps)

def _scatter_add(tgt, idx, src, axis=0):
    return tgt.at[idx].add(src)

def _segment_sum(src, seg, n):
    return jax.ops.segment_sum(src, seg, n)
kernel_name = 'mk_gnn_resnorm_d4_gnn_r64_39b743'

def setup_inputs(seed: int=0):
    np.random.seed(seed)
    _w = jnp.asarray

    def _rec_inputs():
        import jax
        import jax.numpy as jnp
        _gk = jax.random.key(seed)
        x = -0.000202 + 1 * jax.random.normal(jax.random.fold_in(_gk, 1), (50000, 128), jnp.float32)
        src = jax.random.randint(jax.random.fold_in(_gk, 2), (25000,), 0, 50000, jnp.int32)
        dst = jnp.minimum((50000 * jax.random.uniform(jax.random.fold_in(_gk, 3), (25000,)) ** 2.0).astype(jnp.int32), 49999)
        _o = jnp.argsort(dst, stable=True)
        src = src[_o]
        dst = dst[_o]
        edge_weight = 0.000937891 + 0.999965 * jax.random.normal(jax.random.fold_in(_gk, 13), (25000,), jnp.float32)
        edge_weight1 = 0.000614103 + 0.999867 * jax.random.normal(jax.random.fold_in(_gk, 14), (25000, 1), jnp.float32)
        return (x, src, dst, edge_weight, edge_weight1)
    x, src, dst, edge_weight, edge_weight1 = _rec_inputs()

    def _L0_gnn_setup():
        import jax, jax.numpy as jnp
        import numpy as np
        N_NODES = 50000
        NEG_SLOPE = 0.01

        def leaky_relu(x):
            return jnp.where(x >= 0, x, NEG_SLOPE * x)
        key = jax.random.key(seed)
        ks = jax.random.split(key, 6)
        n_edges = 12500
        in_dim, out_dim = (128, 128)
        nf = jax.random.normal(ks[0], (N_NODES, in_dim), dtype=jnp.float32)
        traj = jax.random.normal(ks[1], (n_edges,), dtype=jnp.float32)
        src = jax.random.randint(ks[2], (n_edges,), 0, N_NODES)
        dst = jax.random.randint(ks[3], (n_edges,), 0, N_NODES)
        W_edge = jax.random.normal(ks[4], (2 * in_dim + 1, out_dim), dtype=jnp.float32) / np.sqrt(2 * in_dim + 1)
        b_edge = jnp.zeros((out_dim,), dtype=jnp.float32)
        W_node = jax.random.normal(ks[5], (out_dim + in_dim, out_dim), dtype=jnp.float32) / np.sqrt(out_dim + in_dim)
        b_node = jnp.zeros((out_dim,), dtype=jnp.float32)
        return {'nf': nf, 'traj': traj, 'src': src, 'dst': dst, 'W_edge': W_edge, 'b_edge': b_edge, 'W_node': W_node, 'b_node': b_node}
    _L0_gnn_all = _L0_gnn_setup()
    _L0_gnn_in = {k: v for k, v in _L0_gnn_all.items() if k in ('W_edge', 'b_edge', 'W_node', 'b_node')}
    del _L0_gnn_all

    def _L1_gnn_setup():
        import jax, jax.numpy as jnp
        import numpy as np
        import math
        HEADS = 8
        CH = 16
        SCALE = 1.0 / math.sqrt(CH)

        def _transformer_conv(x, src, dst, qw, qb, kw, kb, vw, vb, sw, sb):
            N = x.shape[0]
            q = (x @ qw + qb).reshape(N, HEADS, CH)
            k = (x @ kw + kb).reshape(N, HEADS, CH)
            v = (x @ vw + vb).reshape(N, HEADS, CH)
            alpha = jnp.sum(q[dst] * k[src], axis=-1) * SCALE
            m = jax.ops.segment_max(alpha, dst, num_segments=N)
            a = jnp.exp(alpha - m[dst])
            denom = jax.ops.segment_sum(a, dst, num_segments=N)
            a = a / denom[dst]
            msg = v[src] * a[:, :, None]
            out = jax.ops.segment_sum(msg, dst, num_segments=N).reshape(N, HEADS * CH)
            return out + x @ sw + sb
        key = jax.random.key(seed)
        ks = jax.random.split(key, 16)
        N, E, IN = (50000, 12500, 128)
        D = HEADS * CH

        def lin(k, fi, fo):
            return jax.random.normal(k, (fi, fo), jnp.float32) / math.sqrt(fi)
        inp = {'x': jax.random.normal(ks[0], (N, IN), jnp.float32), 'edge_index': jax.random.randint(ks[1], (2, E), 0, N, dtype=jnp.int64), 'edge_attr': jax.random.normal(ks[2], (E, 1), jnp.float32), 'q_w0': lin(ks[3], IN, D), 'q_b0': jnp.zeros((D,), jnp.float32), 'k_w0': lin(ks[4], IN, D), 'k_b0': jnp.zeros((D,), jnp.float32), 'v_w0': lin(ks[5], IN, D), 'v_b0': jnp.zeros((D,), jnp.float32), 's_w0': lin(ks[6], IN, D), 's_b0': jnp.zeros((D,), jnp.float32), 'q_w1': lin(ks[7], D, D), 'q_b1': jnp.zeros((D,), jnp.float32), 'k_w1': lin(ks[8], D, D), 'k_b1': jnp.zeros((D,), jnp.float32), 'v_w1': lin(ks[9], D, D), 'v_b1': jnp.zeros((D,), jnp.float32), 's_w1': lin(ks[10], D, D), 's_b1': jnp.zeros((D,), jnp.float32)}
        return inp
    _L1_gnn_all = _L1_gnn_setup()
    _L1_gnn_in = {k: v for k, v in _L1_gnn_all.items() if k in ('q_w0', 'q_b0', 'k_w0', 'k_b0', 'v_w0', 'v_b0', 's_w0', 's_b0', 'q_w1', 'q_b1', 'k_w1', 'k_b1', 'v_w1', 'v_b1', 's_w1', 's_b1')}
    del _L1_gnn_all

    def _L2_gnn_setup():
        import jax, jax.numpy as jnp
        import numpy as np
        N = 100000
        E = 12500
        D = 128
        H = 4
        C = D // H
        EDGE_DIM = 1
        NEG_SLOPE = 0.2
        LN_EPS = 1e-05
        key = jax.random.key(seed)
        ks = jax.random.split(key, 12)
        s = 0.05
        return {'x': jax.random.normal(ks[0], (N, D), jnp.float32), 'edge_index': jax.random.randint(ks[1], (2, E), 0, N, jnp.int32), 'edge_attr': jax.random.uniform(ks[2], (E, EDGE_DIM), jnp.float32), 'W_l': jax.random.normal(ks[3], (D, H * C), jnp.float32) * s, 'b_l': jnp.zeros((H * C,), jnp.float32), 'W_r': jax.random.normal(ks[4], (D, H * C), jnp.float32) * s, 'b_r': jnp.zeros((H * C,), jnp.float32), 'W_e': jax.random.normal(ks[5], (EDGE_DIM, H * C), jnp.float32) * s, 'att': jax.random.normal(ks[6], (H, C), jnp.float32) * s, 'bias': jnp.zeros((H * C,), jnp.float32), 'ln_w': jnp.ones((D,), jnp.float32), 'ln_b': jnp.zeros((D,), jnp.float32)}
    _L2_gnn_all = _L2_gnn_setup()
    _L2_gnn_in = {k: v for k, v in _L2_gnn_all.items() if k in ('W_l', 'b_l', 'W_r', 'b_r', 'W_e', 'att', 'bias', 'ln_w', 'ln_b')}
    del _L2_gnn_all

    def _L3_gnn_setup():
        import jax, jax.numpy as jnp
        import numpy as np
        N_NODES = 50000
        N_EDGES = 12500
        D = 128
        key = jax.random.key(seed)
        k1, k2, k3, k4 = jax.random.split(key, 4)
        x = jax.random.normal(k1, (N_NODES, D), dtype=jnp.float32)
        src = jax.random.randint(k2, (N_EDGES,), 0, N_NODES, dtype=jnp.int64)
        dst = jax.random.randint(k3, (N_EDGES,), 0, N_NODES, dtype=jnp.int64)
        W = jax.random.normal(k4, (D, D), dtype=jnp.float32) * (1.0 / np.sqrt(D))
        return {'x': x, 'src': src, 'dst': dst, 'W': W}
    _L3_gnn_all = _L3_gnn_setup()
    _L3_gnn_in = {k: v for k, v in _L3_gnn_all.items() if k in ('W',)}
    del _L3_gnn_all
    return {'x': x, 'src': src, 'dst': dst, 'edge_weight': edge_weight, 'edge_weight1': edge_weight1, 'L0_gnn_W_edge': _L0_gnn_in['W_edge'], 'L0_gnn_b_edge': _L0_gnn_in['b_edge'], 'L0_gnn_W_node': _L0_gnn_in['W_node'], 'L0_gnn_b_node': _L0_gnn_in['b_node'], 'L1_gnn_q_w0': _L1_gnn_in['q_w0'], 'L1_gnn_q_b0': _L1_gnn_in['q_b0'], 'L1_gnn_k_w0': _L1_gnn_in['k_w0'], 'L1_gnn_k_b0': _L1_gnn_in['k_b0'], 'L1_gnn_v_w0': _L1_gnn_in['v_w0'], 'L1_gnn_v_b0': _L1_gnn_in['v_b0'], 'L1_gnn_s_w0': _L1_gnn_in['s_w0'], 'L1_gnn_s_b0': _L1_gnn_in['s_b0'], 'L1_gnn_q_w1': _L1_gnn_in['q_w1'], 'L1_gnn_q_b1': _L1_gnn_in['q_b1'], 'L1_gnn_k_w1': _L1_gnn_in['k_w1'], 'L1_gnn_k_b1': _L1_gnn_in['k_b1'], 'L1_gnn_v_w1': _L1_gnn_in['v_w1'], 'L1_gnn_v_b1': _L1_gnn_in['v_b1'], 'L1_gnn_s_w1': _L1_gnn_in['s_w1'], 'L1_gnn_s_b1': _L1_gnn_in['s_b1'], 'L2_gnn_W_l': _L2_gnn_in['W_l'], 'L2_gnn_b_l': _L2_gnn_in['b_l'], 'L2_gnn_W_r': _L2_gnn_in['W_r'], 'L2_gnn_b_r': _L2_gnn_in['b_r'], 'L2_gnn_W_e': _L2_gnn_in['W_e'], 'L2_gnn_att': _L2_gnn_in['att'], 'L2_gnn_bias': _L2_gnn_in['bias'], 'L2_gnn_ln_w': _L2_gnn_in['ln_w'], 'L2_gnn_ln_b': _L2_gnn_in['ln_b'], 'L3_gnn_W': _L3_gnn_in['W']}

def reference(x, src, dst, edge_weight, edge_weight1, L0_gnn_W_edge, L0_gnn_b_edge, L0_gnn_W_node, L0_gnn_b_node, L1_gnn_q_w0, L1_gnn_q_b0, L1_gnn_k_w0, L1_gnn_k_b0, L1_gnn_v_w0, L1_gnn_v_b0, L1_gnn_s_w0, L1_gnn_s_b0, L1_gnn_q_w1, L1_gnn_q_b1, L1_gnn_k_w1, L1_gnn_k_b1, L1_gnn_v_w1, L1_gnn_v_b1, L1_gnn_s_w1, L1_gnn_s_b1, L2_gnn_W_l, L2_gnn_b_l, L2_gnn_W_r, L2_gnn_b_r, L2_gnn_W_e, L2_gnn_att, L2_gnn_bias, L2_gnn_ln_w, L2_gnn_ln_b, L3_gnn_W):
    import jax
    import jax.numpy as jnp

    def _L0_gnn_ref(nf, traj, src, dst, W_edge, b_edge, W_node, b_node):
        import jax, jax.numpy as jnp
        import numpy as np
        N_NODES = 50000
        NEG_SLOPE = 0.01

        def leaky_relu(x):
            return jnp.where(x >= 0, x, NEG_SLOPE * x)
        ef = jnp.concatenate([nf[src], nf[dst], traj[:, None]], axis=-1)
        msg = leaky_relu(ef @ W_edge + b_edge)
        red_msg = jax.ops.segment_sum(msg, dst, num_segments=N_NODES)
        in_feat = jnp.concatenate([nf, red_msg], axis=-1)
        out_nf = leaky_relu(in_feat @ W_node + b_node)
        return out_nf

    def _L1_gnn_ref(x, edge_index, edge_attr, q_w0, q_b0, k_w0, k_b0, v_w0, v_b0, s_w0, s_b0, q_w1, q_b1, k_w1, k_b1, v_w1, v_b1, s_w1, s_b1):
        import jax, jax.numpy as jnp
        import numpy as np
        import math
        HEADS = 8
        CH = 16
        SCALE = 1.0 / math.sqrt(CH)

        def _transformer_conv(x, src, dst, qw, qb, kw, kb, vw, vb, sw, sb):
            N = x.shape[0]
            q = (x @ qw + qb).reshape(N, HEADS, CH)
            k = (x @ kw + kb).reshape(N, HEADS, CH)
            v = (x @ vw + vb).reshape(N, HEADS, CH)
            alpha = jnp.sum(q[dst] * k[src], axis=-1) * SCALE
            m = jax.ops.segment_max(alpha, dst, num_segments=N)
            a = jnp.exp(alpha - m[dst])
            denom = jax.ops.segment_sum(a, dst, num_segments=N)
            a = a / denom[dst]
            msg = v[src] * a[:, :, None]
            out = jax.ops.segment_sum(msg, dst, num_segments=N).reshape(N, HEADS * CH)
            return out + x @ sw + sb
        src, dst = (edge_index[0], edge_index[1])
        h = _transformer_conv(x, src, dst, q_w0, q_b0, k_w0, k_b0, v_w0, v_b0, s_w0, s_b0)
        h = jax.nn.relu(h)
        h = _transformer_conv(h, src, dst, q_w1, q_b1, k_w1, k_b1, v_w1, v_b1, s_w1, s_b1)
        return h

    def _L2_gnn_ref(x, edge_index, edge_attr, W_l, b_l, W_r, b_r, W_e, att, bias, ln_w, ln_b):
        import jax, jax.numpy as jnp
        import numpy as np
        N = 100000
        E = 12500
        D = 128
        H = 4
        C = D // H
        EDGE_DIM = 1
        NEG_SLOPE = 0.2
        LN_EPS = 1e-05
        n = x.shape[0]
        loops = jnp.arange(n, dtype=edge_index.dtype)
        src = jnp.concatenate([edge_index[0], loops])
        tgt = jnp.concatenate([edge_index[1], loops])
        ea = jnp.concatenate([edge_attr, jnp.broadcast_to(edge_attr.mean(0), (n, edge_attr.shape[1]))], axis=0)
        x_l = (x @ W_l + b_l).reshape(n, H, C)
        x_r = (x @ W_r + b_r).reshape(n, H, C)
        e_emb = (ea @ W_e).reshape(-1, H, C)
        x_j = x_l[src]
        m = jax.nn.leaky_relu(x_j + x_r[tgt] + e_emb, NEG_SLOPE)
        logits = jnp.einsum('ehc,hc->eh', m, att)
        lmax = jax.ops.segment_max(logits, tgt, num_segments=n)
        lmax = jnp.where(jnp.isfinite(lmax), lmax, 0.0)
        ex = jnp.exp(logits - lmax[tgt])
        den = jax.ops.segment_sum(ex, tgt, num_segments=n)
        alpha = ex / (den[tgt] + 1e-16)
        out = jax.ops.segment_sum(alpha[..., None] * x_j, tgt, num_segments=n)
        out = out.reshape(n, H * C) + bias
        out = jax.nn.gelu(out, approximate=False)
        h = out + x
        mu = jnp.mean(h, axis=-1, keepdims=True)
        var = jnp.mean((h - mu) ** 2, axis=-1, keepdims=True)
        return (h - mu) * jax.lax.rsqrt(var + LN_EPS) * ln_w + ln_b

    def _L3_gnn_ref(x, src, dst, W):
        import jax, jax.numpy as jnp
        import numpy as np
        N_NODES = 50000
        N_EDGES = 12500
        D = 128
        h_in = x
        agg = jax.ops.segment_sum(x[src], dst, num_segments=N_NODES)
        h = agg @ W.T
        h = jax.nn.relu(h)
        h = h + h_in
        return h
    edge_index = jnp.stack([src, dst])
    x = _layernorm(x + _L0_gnn_ref(x, edge_weight, src, dst, L0_gnn_W_edge, L0_gnn_b_edge, L0_gnn_W_node, L0_gnn_b_node), axis=-1)
    x = _layernorm(x + _L1_gnn_ref(x, edge_index, edge_weight1, L1_gnn_q_w0, L1_gnn_q_b0, L1_gnn_k_w0, L1_gnn_k_b0, L1_gnn_v_w0, L1_gnn_v_b0, L1_gnn_s_w0, L1_gnn_s_b0, L1_gnn_q_w1, L1_gnn_q_b1, L1_gnn_k_w1, L1_gnn_k_b1, L1_gnn_v_w1, L1_gnn_v_b1, L1_gnn_s_w1, L1_gnn_s_b1), axis=-1)
    x = _layernorm(x + _L2_gnn_ref(x, edge_index, edge_weight1, L2_gnn_W_l, L2_gnn_b_l, L2_gnn_W_r, L2_gnn_b_r, L2_gnn_W_e, L2_gnn_att, L2_gnn_bias, L2_gnn_ln_w, L2_gnn_ln_b), axis=-1)
    x = _layernorm(x + _L3_gnn_ref(x, src, dst, L3_gnn_W), axis=-1)
    return x

_drawn_inputs = setup_inputs


def setup_inputs(seed=0):
    import zlib

    import numpy as np

    out = dict(_drawn_inputs(seed))
    spreads = {'L0_gnn_b_edge': (0.0, 0.362),
     'L0_gnn_b_node': (0.0, 0.1),
     'L1_gnn_q_b0': (0.0, 0.8),
     'L1_gnn_k_b0': (0.0, 0.8),
     'L1_gnn_v_b0': (0.0, 0.275),
     'L1_gnn_s_b0': (0.0, 0.1),
     'L1_gnn_q_b1': (0.0, 0.8),
     'L1_gnn_k_b1': (0.0, 0.8),
     'L1_gnn_v_b1': (0.0, 0.1),
     'L1_gnn_s_b1': (0.0, 0.1),
     'L2_gnn_b_l': (0.0, 0.1),
     'L2_gnn_b_r': (0.0, 0.8),
     'L2_gnn_bias': (0.0, 0.1),
     'L2_gnn_ln_w': (1.0, 0.2),
     'L2_gnn_ln_b': (0.0, 0.1)}
    factors = {'edge_weight': 5.431,
     'edge_weight1': 8.0,
     'L2_gnn_W_r': 8.0,
     'L2_gnn_W_e': 8.0,
     'L2_gnn_att': 8.0}
    for name, (base, spread) in spreads.items():
        noise = np.random.default_rng([zlib.crc32(name.encode()), seed]).standard_normal(out[name].shape)
        drawn = base * np.exp(spread * noise) if base else spread * noise
        out[name] = jnp.asarray(drawn.astype(out[name].dtype))
    for name, factor in factors.items():
        out[name] = (out[name] * factor).astype(out[name].dtype)
    return out
```

```python
from contextlib import ExitStack

import concourse.bass as bass
from concourse import mybir
from concourse.alu_op_type import AluOpType as ALU

F32 = mybir.dt.float32
BF16 = mybir.dt.bfloat16
I32 = mybir.dt.int32
U8 = mybir.dt.uint8
ACT = mybir.ActivationFunctionType
AX_X = mybir.AxisListType.X

P = 128
NODES, EDGES = 50000, 25000
TILE = 512
STEPS = 50
EDGE_ROWS = STEPS * TILE
NODE_ROWS = 2 * STEPS * TILE
TABLE_ROWS = NODE_ROWS + EDGE_ROWS
COLS = EDGE_ROWS // P
HALF = COLS // 2
FAR = float(2 ** 100)
EPS = 1e-5
DEN_EPS = 1e-16
LN_EXP = "natural_log_exp_and_others"
PEEL = 6


class Tile:

    def __init__(self, i, c):
        self.i, self.c = i, c
        self.n = 2 * i + c
        self.slot = c % 2
        self.half = i + (c - c % 2) // 2


class Step:

    def __init__(self, i, c):
        self.i, self.c = i, c

    def tile(self, lag):
        t = Tile(self.i, self.c - lag)
        return None if isinstance(t.n, int) and not 0 <= t.n < STEPS else t

    def group(self, lag):
        g = Tile(self.i, self.c - lag)
        if isinstance(g.n, int) and not 0 <= g.n <= STEPS:
            return None, 0, 0
        return g, (0 if self.tile(lag) else 2), (3 if self.tile(lag + 1) else 2)


def run_steps(eng, lag, step):
    for c in range(PEEL):
        step(Step(0, c))
    with eng.Fori(PEEL // 2, STEPS // 2) as i:
        step(Step(i, 0))
        step(Step(i, 1))
    for c in range(STEPS, STEPS + lag):
        step(Step(0, c))


def wait(eng, sem, value):
    if not (isinstance(value, int) and value <= 0):
        eng.wait_ge(sem, value)


def quarters(ap):
    return [ap[:, P * j:P * (j + 1)] for j in range(TILE // P)]


def wait_for_dma(pool, sem, value, starts):
    pool.wait_ge(sem, value)
    pool.sem_inc(starts, 1)


def by_row(ap):
    return ap.rearrange("p (j f) -> p j f", f=P)


def edge_rows(table, n):
    return table[bass.ds(NODE_ROWS + n * TILE, TILE), :].rearrange("(j p) f -> p j f", p=P)


def node_rows(table, n):
    return table[bass.ds(n * 2 * TILE, 2 * TILE), :].rearrange("(b p j) f -> p b (j f)", b=2, p=P)


class Held:
    pass


def names_of_weights():
    return ["w_src", "w_dst", "w_node", "w_red", "q0", "k0", "v0", "s0", "q1", "k1", "v1", "s1",
            "w_l", "w_r", "w3t", "ident", "center", "heads8", "blocks4"]


def names_of_columns():
    return ["b_edge", "b_node", "q_b0", "k_b0", "v_b0", "s_b0", "q_b1", "k_b1", "v_b1",
            "s_b1",            "b_l", "b_r", "w_e", "att", "g_bias", "ln_w", "ln_b"]


def setup(nc, io, h):
    with ExitStack() as ctx:
        ctx.enter_context(nc.cleanup_on_exit())
        sem = lambda name: nc.alloc_semaphore("i_" + name)
        sb = lambda name, shape, dt=F32: ctx.enter_context(nc.sbuf_tensor("i_" + name, shape, dt))
        dstb = sb("dstb", [P, 2, TILE + 1], I32)
        dst_next = sb("dst_next", [P, COLS], I32)
        same = sb("same", [P, COLS], I32)
        at_end = sb("at_end", [P, COLS], I32)
        rowno = sb("rowno", [P, COLS], I32)
        nodeno = sb("nodeno", [P, NODE_ROWS // P], I32)
        ixs = sb("ixs", [P, 2, 4], I32)
        rns = sb("rns", [P, 2, 4], I32)
        ew1 = sb("ew1", [P, COLS], F32)
        ewsum = sb("ewsum", [P, 1], F32)
        ones = sb("ones", [P, P], F32)
        rowm = sb("rowm", [P, 2], F32)
        psm = ctx.enter_context(nc.psum_tensor("psm", [P, TILE], F32))
        rev, rev_before = sb("rev", [HALF, 2 * P], I32), sb("rev_before", [HALF, 2 * P], I32)
        rev_row = sb("rev_row", [HALF, 2 * P], I32)
        goes_on, begins, zeros = (sb(n, [HALF, 2 * P]) for n in ("goes_on", "begins", "zeros"))
        found, unfound, flip = sb("found", [HALF, 2 * P]), sb("unfound", [HALF, 2 * P]), sb("flip", [P, P])
        ends_row, carry, carry_col = sb("ends_row", [1, 2 * COLS]), sb("carry", [1, COLS + 1]), sb("carry_col", [HALF, 2])
        turned_rows = sb("turned_rows", [P, COLS])
        psr, psc, psy = (ctx.enter_context(nc.psum_tensor("i_" + n, [P, TILE], F32)) for n in ("psr", "psc", "psy"))
        (chunks_ready, chunk_ends, carry_ready, carry_cols, whole_ready, rows_turned, rows_kept,
         rows_flipped) = map(sem, ("chunks_ready", "chunk_ends", "carry_ready", "carry_cols", "whole_ready",
                                   "rows_turned", "rows_kept", "rows_flipped"))
        loaded, numbered, table_init, ends_ready = map(sem, ["loaded", "numbered", "table_init", "ends_ready"])
        dst_landed = [sem(f"dst_landed{s}") for s in range(2)]
        cont_ready, far_ready, chain = map(sem, ["cont_ready", "far_ready", "chain"])
        far_stored, starts, slot_ready, sum_ready, mean_ready, rows_zero = map(sem, ["far_stored", "starts", "slot_ready", "sum_ready", "mean_ready", "rows_zero"])
        scattered = [sem(f"scattered{s}") for s in range(2)]
        block = ctx.enter_context(nc.Block())
        n_loads = [0]

        @block.sync
        def _(sp):
            def load(dst, src):
                sp.dma_start(dst, src).then_inc(loaded, 16)
                n_loads[0] += 16

            for name in names_of_weights():
                load(h.w[name][:, :], io[name])
            for k, name in enumerate(names_of_columns()):
                load(h.cols[:, k:k + 1], io[name])
            sp.wait_ge(rows_zero, 1)
            load(h.w_edge_row[0:1, :], io["w_edge_row"])
            load(h.w_e_row[0:1, :], io["w_e_row"])
            load(h.s_b0[:, :], io["s_row0"].to_broadcast([P, P]))
            load(h.s_b1c[:, :], io["s_row1"].to_broadcast([P, P]))
            load(h.src_i[:, :], io["src"])
            load(h.dst_i[:, :], io["dst"])
            load(dst_next[:, :], io["dst_next"])
            load(ew1[:, :], io["ew1_cols"])
            load(rev[:, :], io["rev"])
            load(rev_before[:, :], io["rev_before"])
            load(flip[:, :], io["flip"])
            sp.wait_ge(numbered, 1)
            sp.dma_start(io["row_of"].rearrange("(p c) o -> p (c o)", p=P), nodeno[:, :]).then_inc(table_init, 16)

            def masks(t):
                now = t.tile(0)
                wait(sp, far_ready, now.n - 1)
                sp.dma_start(dstb[:, now.slot, :],
                             io["dst_flat"][:, bass.ds(now.n * TILE, TILE + 1)].to_broadcast([P, TILE + 1])
                             ).then_inc(dst_landed[now.slot], 16)

            run_steps(sp, 0, masks)
            sp.wait_ge(far_ready, STEPS)
            sp.dma_start(io["far"], h.far[0:1, :]).then_inc(far_stored, 16)
            sp.wait_ge(far_stored, 16)

        @block.vector
        def _(dve):
            links = [0]

            def link(ins):
                links[0] += 1
                ins.then_inc(chain, 1)
                dve.wait_ge(chain, links[0])

            nc.vector.memset(h.w_edge_row[:, :], 0.0)
            nc.vector.memset(h.w_e_row[:, :], 0.0).then_inc(rows_zero, 1)
            nc.vector.memset(h.eps[:, :], EPS)
            nc.vector.memset(h.eps4[:, :], EPS / 4)
            nc.vector.memset(h.avg[:, :], 1.0 / P)
            nc.vector.memset(h.den_eps[:, :], DEN_EPS)
            link(nc.vector.memset(ones[:, :], 1.0))
            dve.wait_ge(loaded, n_loads[0])
            link(nc.vector.tensor_tensor(same[:, :], h.dst_i[:, :], dst_next[:, :], ALU.is_equal))
            nc.vector.scalar_tensor_tensor(out=at_end[:, :], in0=same[:, :], scalar=float(1 << 20),
                                           in1=h.dst_i[:, :], op0=ALU.mult, op1=ALU.add).then_inc(ends_ready, 1)
            dve.wait_ge(ends_ready, 1)
            link(nc.vector.tensor_copy(h.end_i[:, :], at_end[:, :]))
            link(nc.vector.tensor_reduce(rowm[:, 0:1], h.w["s1"][:, :], AX_X, ALU.add))
            link(nc.vector.tensor_scalar(rowm[:, 1:2], rowm[:, 0:1], -1.0 / P, None, ALU.mult))
            link(nc.vector.tensor_scalar(h.s1c[:, :], h.w["s1"][:, :], rowm[:, 1:2], None, ALU.add))
            link(nc.vector.tensor_reduce(rowm[:, 0:1], h.s_b1c[:, :], AX_X, ALU.add))
            link(nc.vector.tensor_scalar(rowm[:, 1:2], rowm[:, 0:1], -1.0 / P, None, ALU.mult))
            link(nc.vector.tensor_scalar(h.s_b1c[:, :], h.s_b1c[:, :], rowm[:, 1:2], None, ALU.add))
            for k in range(2):
                link(nc.vector.tensor_tensor(h.b_vs[:, k:k + 1], h.col(f"v_b{k}"), h.col(f"s_b{k}"), ALU.add))
            link(nc.vector.tensor_tensor(h.w_lr[:, :], h.w["w_l"][:, :], h.w["w_r"][:, :], ALU.add))
            link(nc.vector.tensor_scalar(h.att_m[:, :], h.w["blocks4"][:, :], h.col("att"), None, ALU.mult))
            link(nc.vector.tensor_scalar(h.x01b_node[:, :], h.col("b_node"), 0.01, None, ALU.mult))
            link(nc.vector.tensor_scalar(h.x01b_edge[:, :], h.col("b_edge"), 0.01, None, ALU.mult))
            link(nc.vector.tensor_tensor(h.blr[:, :], h.col("b_l"), h.col("b_r"), ALU.add))
            link(nc.vector.tensor_scalar(h.x2blr[:, :], h.blr[:, :], 0.2, None, ALU.mult))
            link(nc.vector.tensor_tensor(h.bl_out[:, :], h.col("b_l"), h.col("g_bias"), ALU.add))
            dve.wait_ge(numbered, 3)
            link(nc.vector.memset(zeros[:, :], 0.0))
            link(nc.vector.memset(carry[:, 0:1], 0.0))
            link(nc.vector.tensor_tensor(goes_on[:, :], rev[:, :], rev_before[:, :], ALU.is_equal))
            link(nc.vector.tensor_scalar(begins[:, :], goes_on[:, :], -1.0, 1.0, ALU.mult, ALU.add))
            link(nc.vector.tensor_tensor(begins[:, :], begins[:, :], rev_row[:, :], ALU.mult))
            for g in range(2):
                part = slice(P * g, P * (g + 1))
                nc.vector.tensor_tensor_scan(found[:, part], goes_on[:, part], begins[:, part], 0.0,
                                             ALU.mult, ALU.add).then_inc(chunks_ready, 1)
                nc.vector.tensor_tensor_scan(unfound[:, part], goes_on[:, part], zeros[:, part], 1.0,
                                             ALU.mult, ALU.add).then_inc(chunks_ready, 1)
            dve.wait_ge(chunk_ends, 1)
            link(nc.vector.tensor_copy(ends_row[:, :], psr[0:1, 0:2 * COLS]))
            nc.vector.tensor_tensor_scan(carry[:, 1:COLS + 1], ends_row[:, COLS:2 * COLS], ends_row[:, 0:COLS], 0.0,
                                         ALU.mult, ALU.add).then_inc(carry_ready, 1)
            dve.wait_ge(carry_cols, 1)
            link(nc.vector.tensor_copy(carry_col[:, :], psc[0:HALF, 0:2]))
            for g in range(2):
                part = slice(P * g, P * (g + 1))
                nc.vector.scalar_tensor_tensor(out=found[:, part], in0=unfound[:, part], scalar=carry_col[:, g:g + 1],
                                               in1=found[:, part], op0=ALU.mult, op1=ALU.add).then_inc(whole_ready, 1)
            dve.wait_ge(rows_turned, 1)
            nc.vector.tensor_copy(turned_rows[:, :], psy[:, 0:COLS]).then_inc(rows_kept, 1)
            dve.wait_ge(rows_flipped, 1)
            link(nc.vector.tensor_copy(h.dst_row[:, :], psr[:, 0:COLS]))
            nc.vector.tensor_reduce(ewsum[:, :], ew1[:, :], AX_X, ALU.add).then_inc(sum_ready, 1)
            dve.wait_ge(mean_ready, 1)
            link(nc.vector.tensor_scalar(rowm[:, 0:1], psm[:, 0:1], 1.0 / EDGES, None, ALU.mult))
            link(nc.vector.scalar_tensor_tensor(out=h.b_self[:, :], in0=rowm[:, 0:1], scalar=h.col("w_e"),
                                                in1=h.blr[:, :], op0=ALU.mult, op1=ALU.add))
            link(nc.vector.tensor_scalar(h.x2b_self[:, :], h.b_self[:, :], 0.2, None, ALU.mult))

            def masks(t):
                now = t.tile(0)
                dve.wait_ge(dst_landed[now.slot], 16 * (now.half + 1))
                here = bass.ds(now.n * TILE, TILE)
                nc.vector.tensor_tensor(h.cont[:, here], dstb[:, now.slot, 1:TILE + 1], dstb[:, now.slot, 0:TILE],
                                        ALU.is_equal).then_inc(cont_ready, 1)
                dve.wait_ge(cont_ready, now.n + 1)
                nc.vector.tensor_scalar(h.far[:, here], h.cont[:, here], -1.0, FAR, ALU.add,
                                        ALU.mult).then_inc(far_ready, 1)

            run_steps(dve, 0, masks)

        @block.tensor
        def _(pe):
            pe.wait_ge(loaded, n_loads[0])
            pe.wait_ge(chunks_ready, 4)
            ident, one = h.w["ident"], ones[0:1, 0:1]
            for k, x in enumerate((found, unfound)):
                for g in range(2):
                    at = COLS * k + HALF * g
                    ins = nc.tensor.matmul(psr[0:1, at:at + HALF], x[:, P * (g + 1) - 1:P * (g + 1)],
                                           ident[0:HALF, 0:HALF], start=True, stop=True)
            ins.then_inc(chunk_ends, 1)
            pe.wait_ge(carry_ready, 1)
            for g in range(2):
                ins = nc.tensor.matmul(psc[0:HALF, g:g + 1], carry[:, HALF * g:HALF * (g + 1)], one,
                                       start=True, stop=True)
            ins.then_inc(carry_cols, 1)
            pe.wait_ge(whole_ready, 2)
            for g in range(2):
                ins = nc.tensor.matmul(psy[:, HALF * (1 - g):HALF * (2 - g)], found[:, P * g:P * (g + 1)],
                                       flip[0:HALF, P - HALF:P], start=True, stop=True)
            ins.then_inc(rows_turned, 1)
            pe.wait_ge(rows_kept, 1)
            nc.tensor.matmul(psr[:, 0:COLS], flip[:, :], turned_rows[:, :], start=True, stop=True).then_inc(rows_flipped, 1)
            pe.wait_ge(sum_ready, 1)
            nc.tensor.matmul(psm[:, 0:1], ones[:, :], ewsum[:, :], start=True, stop=True).then_inc(mean_ready, 1)

        @block.gpsimd
        def _(pool):
            nc.gpsimd.iota(nodeno[:, :], [[1, NODE_ROWS // P]], base=0,
                           channel_multiplier=NODE_ROWS // P).then_inc(numbered, 1)
            nc.gpsimd.iota(rowno[:, :], [[P, COLS]], base=NODE_ROWS, channel_multiplier=1).then_inc(numbered, 1)
            nc.gpsimd.iota(rev_row[:, :], [[-HALF * P, 2], [-1, P]], base=TABLE_ROWS - 1,
                           channel_multiplier=-P).then_inc(numbered, 1)
            pool.wait_ge(ends_ready, 1)
            pool.wait_ge(numbered, 3)
            pool.wait_ge(table_init, 16)

            def scatter(t):
                now = t.tile(0)
                wait(pool, scattered[now.slot], 64 * now.half)
                nc.gpsimd.tensor_copy(ixs[:, now.slot, :], at_end[:, bass.ds(now.n * 4, 4)]).then_inc(slot_ready, 1)
                nc.gpsimd.tensor_copy(rns[:, now.slot, :], rowno[:, bass.ds(now.n * 4, 4)]).then_inc(slot_ready, 1)
                wait_for_dma(pool, slot_ready, 2 * now.n + 2, starts)
                for j in range(4):
                    pool.indirect_dma_start(
                        out=io["row_of"], out_offset=bass.IndirectOffsetOnAxis(ap=ixs[:, now.slot, j:j + 1], axis=0),
                        in_=rns[:, now.slot, j:j + 1], in_offset=None,
                        bounds_check=NODE_ROWS - 1, oob_is_err=False).then_inc(scattered[now.slot], 16)

            run_steps(pool, 0, scatter)
            for s in range(2):
                pool.wait_ge(scattered[s], 64 * STEPS // 2)


def norm_sum(nc, dve, g, a, b, sq, var, sq_ready, var_ready, rstd_ready):
    dve.wait_ge(sq_ready, g.n + 1)
    wait(dve, rstd_ready, g.n - 1)
    nc.vector.tensor_reduce(var[:, g.slot, 4 * a:4 * b], by_row(sq[:, a:b, :].rearrange("p b n -> p (b n)")),
                            AX_X, ALU.add).then_inc(var_ready, 1)


def norm_scale(nc, act, h, g, a, b, var, lnv, rstd, var_ready, lnv_ready, rstd_ready, out_ready):
    act.wait_ge(var_ready, g.n + 1)
    wait(act, rstd_ready, g.n)
    nc.scalar.activation(lnv[:, 4 * a:4 * b], var[:, g.slot, 4 * a:4 * b], ACT.Ln, bias=h.eps[:, :],
                         scale=1.0 / P).then_inc(lnv_ready, 1)
    act.wait_ge(lnv_ready, g.n + 1)
    wait(act, out_ready, g.n - 1)
    nc.scalar.activation(rstd[:, g.slot, 4 * a:4 * b], lnv[:, 4 * a:4 * b], ACT.Exp,
                         scale=-0.5).then_inc(rstd_ready, 1)


def norm_apply(nc, dve, t, g, a, b, cen, rstd, xo, rstd_ready, out_ready, node_stored, edge_stored):
    dve.wait_ge(rstd_ready, g.n + 1)
    free_of_stores(dve, t, g, a, b, node_stored, edge_stored)
    scale = rstd[:, g.slot, 4 * a:4 * b].rearrange("p (b o) -> p b o", o=1).to_broadcast([P, 4 * (b - a), P])
    nc.vector.tensor_tensor(by_row(xo[:, g.slot, a:b, :].rearrange("p b n -> p (b n)")),
                            by_row(cen[:, g.slot, a:b, :].rearrange("p b n -> p (b n)")),
                            scale, ALU.mult).then_inc(out_ready, 1)


def free_of_stores(eng, t, g, a, b, node_stored, edge_stored):
    if a == 0:
        wait(eng, node_stored[g.slot], 16 * g.half)
    if b == 3:
        e = Tile(g.i, g.c - 1)
        wait(eng, edge_stored[e.slot], 16 * e.half)


def store_group(sp, g, a, b, t, table, xo, out_ready, node_stored, edge_stored):
    if not g:
        return
    sp.wait_ge(out_ready, g.n + 1)
    if a == 0:
        sp.dma_start(node_rows(table, g.n), xo[:, g.slot, 0:2, :]).then_inc(node_stored[g.slot], 16)
    if b == 3:
        e = Tile(g.i, g.c - 1)
        sp.dma_start(edge_rows(table, e.n), by_row(xo[:, g.slot, 2, :])).then_inc(edge_stored[e.slot], 16)


def all_stored(sp, node_stored, edge_stored):
    for s in range(2):
        sp.wait_ge(node_stored[s], 16 * STEPS // 2)
        sp.wait_ge(edge_stored[s], 16 * STEPS // 2)


def layer0(nc, io, h):
    with ExitStack() as ctx:
        ctx.enter_context(nc.cleanup_on_exit())
        sem = lambda name: nc.alloc_semaphore("e_" + name)
        sb = lambda name, shape, dt=F32: ctx.enter_context(nc.sbuf_tensor(name, shape, dt))
        bank = lambda name: ctx.enter_context(nc.psum_tensor(name, [P, TILE], F32))
        x0, x1 = io["x0"], io["x1"]
        ix = sb("ix", [P, 2, 8], I32)
        found = sb("found", [P, 2, 4], I32)
        xs, xd = sb("xs", [P, 2, TILE]), sb("xd", [P, 2, TILE])
        xsT, xdT = sb("xsT", [P, 2, TILE]), sb("xdT", [P, 2, TILE])
        xn, xnT = sb("xn", [P, 2, 2, TILE]), sb("xnT", [P, 2, 2, TILE])
        erow = sb("erow", [P, 2, TILE])
        z01, msg, red = sb("z01", [P, TILE]), sb("msg", [P, TILE]), sb("red", [P, 2, TILE])
        y01, lr, tT = sb("y01", [P, 3, TILE]), sb("lr", [P, 3, TILE]), sb("tT", [P, 3, TILE])
        cen, sq = sb("cen", [P, 2, 3, TILE]), sb("sq", [P, 3, TILE])
        var, lnv, rstd = sb("var", [P, 2, 12]), sb("lnv", [P, 12]), sb("rstd", [P, 2, 12])
        xo = sb("xo", [P, 2, 3, TILE])
        psT = [bank(f"psT{k}") for k in range(2)]
        psZ = bank("psZ")
        psY = [bank(f"psY{k}") for k in range(2)]
        psE = [bank(f"psE{k}") for k in range(2)]
        src_landed, dst_landed, node_landed, erow_landed, found_landed, node_stored, edge_stored = [
            [sem(f"{n}{s}") for s in range(2)] for n in
            ("src_landed", "dst_landed", "node_landed", "erow_landed", "found_landed", "node_stored", "edge_stored")]
        (starts, ix_ready, found_kept, turned, turned_sb, erow_zero, z_ready, z01_ready, msg_ready, red_ready,
         yn_ready, ye_ready, yn01_ready, ye01_ready, lrn_ready, lre_ready, tn_ready, te_ready,
         en_ready, ee_ready, cn_ready, ce_ready, sq_ready, var_ready, lnv_ready, rstd_ready, out_ready) = map(sem, (
             "starts", "ix_ready", "found_kept", "turned", "turned_sb", "erow_zero", "z_ready", "z01_ready", "msg_ready",
             "red_ready", "yn_ready", "ye_ready", "yn01_ready", "ye01_ready", "lrn_ready", "lre_ready", "tn_ready",
             "te_ready", "en_ready", "ee_ready", "cn_ready", "ce_ready", "sq_ready", "var_ready", "lnv_ready",
             "rstd_ready", "out_ready"))
        block = ctx.enter_context(nc.Block())

        @block.gpsimd
        def _(pool):
            def step(t):
                now, last = t.tile(0), t.tile(1)
                if now:
                    s = now.slot
                    wait(pool, found_landed[s], 64 * now.half)
                    wait(pool, src_landed[s], 64 * now.half)
                    wait(pool, dst_landed[s], 64 * now.half)
                    nc.gpsimd.tensor_copy(ix[:, s, 0:4], h.src_i[:, bass.ds(now.n * 4, 4)]).then_inc(ix_ready, 1)
                    nc.gpsimd.tensor_copy(ix[:, s, 4:8], h.dst_i[:, bass.ds(now.n * 4, 4)]).then_inc(ix_ready, 1)
                    wait(pool, turned, 4 * now.n - 6)
                    wait(pool, found_kept, now.n - 1)
                    wait_for_dma(pool, ix_ready, 2 * now.n + 2, starts)
                    for j in range(4):
                        for k, (rows, landed) in enumerate(((xs, src_landed), (xd, dst_landed))):
                            at = bass.IndirectOffsetOnAxis(ap=ix[:, s, 4 * k + j:4 * k + j + 1], axis=0)
                            pool.indirect_dma_start(out=quarters(rows[:, s, :])[j], out_offset=None, in_=x0,
                                                    in_offset=at).then_inc(landed[s], 16)
                    for j in range(4):
                        at = bass.IndirectOffsetOnAxis(ap=ix[:, s, j:j + 1], axis=0)
                        pool.indirect_dma_start(out=found[:, s, j:j + 1], out_offset=None, in_=io["row_of"],
                                                in_offset=at).then_inc(found_landed[s], 16)
                if last:
                    pool.wait_ge(found_landed[last.slot], 64 * (last.half + 1))
                    nc.gpsimd.tensor_copy(h.src_row[:, bass.ds(last.n * 4, 4)],
                                          found[:, last.slot, :]).then_inc(found_kept, 1)

            run_steps(pool, 1, step)

        @block.sync
        def _(sp):
            sp.wait_ge(erow_zero, 1)

            def step(t):
                now, (g, a, b) = t.tile(0), t.group(2)
                if now:
                    s = now.slot
                    wait(sp, turned, 4 * now.n - 4)
                    sp.dma_start(xn[:, s, :, :], node_rows(x0, now.n)).then_inc(node_landed[s], 16)
                    wait(sp, z_ready, now.n - 1)
                    sp.dma_start(erow[0:1, s, :], io["ew"][:, bass.ds(now.n * TILE, TILE)]).then_inc(erow_landed[s], 16)
                store_group(sp, g, a, b, t, x1, xo, out_ready, node_stored, edge_stored)

            run_steps(sp, 3, step)
            all_stored(sp, node_stored, edge_stored)

        @block.tensor
        def _(pe):
            def turn(k, now, rows, landed, count):
                pe.wait_ge(landed, count)
                wait(pe, turned_sb, 4 * now.n + k - 1)
                for o, x in zip(quarters(psT[k % 2]), quarters(rows)):
                    ins = nc.tensor.transpose(o, x, h.w["ident"][:, :])
                ins.then_inc(turned, 1)

            def centred(dst, src):
                for o, x in zip(quarters(dst), quarters(src)):
                    ins = nc.tensor.matmul(o, x, h.w["center"][:, :], start=True, stop=True)
                return ins

            def step(t):
                now, last = t.tile(0), t.tile(1)
                if now:
                    s = now.slot
                    turn(0, now, xs[:, s, :], src_landed[s], 64 * (now.half + 1))
                    turn(1, now, xd[:, s, :], dst_landed[s], 64 * (now.half + 1))
                if last:
                    pe.wait_ge(red_ready, last.n + 1)
                    wait(pe, lrn_ready, 2 * last.n + 1)
                    nc.tensor.matmul(psY[0][:, :], h.w["w_node"][:, :], xdT[:, last.slot, :], start=True, stop=False)
                    nc.tensor.matmul(psY[0][:, :], h.w["w_red"][:, :], red[:, last.slot, :],
                                     start=False, stop=True).then_inc(ye_ready, 1)
                if now:
                    pe.wait_ge(turned_sb, 4 * now.n + 2)
                    pe.wait_ge(erow_landed[s], 16 * (now.half + 1))
                    wait(pe, msg_ready, now.n)
                    nc.tensor.matmul(psZ[:, :], h.w["w_src"][:, :], xsT[:, s, :], start=True, stop=False)
                    nc.tensor.matmul(psZ[:, :], h.w["w_dst"][:, :], xdT[:, s, :], start=False, stop=False)
                    nc.tensor.matmul(psZ[:, :], h.w_edge_row[:, :], erow[:, s, :],
                                     start=False, stop=True).then_inc(z_ready, 1)
                    turn(2, now, xn[:, s, 0, :], node_landed[s], 16 * (now.half + 1))
                    turn(3, now, xn[:, s, 1, :], node_landed[s], 16 * (now.half + 1))
                    for b in range(2):
                        pe.wait_ge(turned_sb, 4 * now.n + 3 + b)
                        if b == 0:
                            wait(pe, lre_ready, now.n)
                        else:
                            wait(pe, lrn_ready, 2 * now.n)
                        nc.tensor.matmul(psY[b][:, :], h.w["w_node"][:, :], xnT[:, s, b, :],
                                         start=True, stop=True).then_inc(yn_ready, 1)
                if last:
                    pe.wait_ge(te_ready, last.n + 1)
                    wait(pe, cn_ready, 2 * last.n + 1)
                    centred(psE[0], tT[:, 2, :]).then_inc(ee_ready, 1)
                if now:
                    for b in range(2):
                        pe.wait_ge(tn_ready, 2 * now.n + 1 + b)
                        if b == 0:
                            wait(pe, ce_ready, now.n)
                        else:
                            wait(pe, cn_ready, 2 * now.n)
                        centred(psE[b], tT[:, b, :]).then_inc(en_ready, 1)

            run_steps(pe, 1, step)

        @block.scalar
        def _(act):
            nc.scalar.preload_act_table_set(LN_EXP)

            def turned_to(dst, now, k):
                act.wait_ge(turned, 4 * now.n + k + 1)
                if k == 0:
                    wait(act, z_ready, now.n - 1)
                elif k == 1:
                    wait(act, te_ready, now.n - 1)
                else:
                    wait(act, tn_ready, 2 * now.n - 4 + k - 1)
                nc.scalar.activation(dst, psT[k % 2][:, :], ACT.Copy).then_inc(turned_sb, 1)

            def step(t):
                now, last, (g, a, b) = t.tile(0), t.tile(1), t.group(1)
                if now:
                    s = now.slot
                    turned_to(xsT[:, s, :], now, 0)
                    turned_to(xdT[:, s, :], now, 1)
                if g:
                    if a == 0:
                        act.wait_ge(cn_ready, 2 * g.n + 2)
                    if b == 3:
                        act.wait_ge(ce_ready, g.n)
                    wait(act, var_ready, g.n)
                    nc.scalar.activation(sq[:, a:b, :], cen[:, g.slot, a:b, :], ACT.Square).then_inc(sq_ready, 1)
                if last:
                    act.wait_ge(ye_ready, last.n + 1)
                    wait(act, lre_ready, last.n)
                    nc.scalar.activation(y01[:, 2, :], psY[0][:, :], ACT.Identity, bias=h.x01b_node[:, :],
                                         scale=0.01).then_inc(ye01_ready, 1)
                if now:
                    act.wait_ge(z_ready, now.n + 1)
                    wait(act, msg_ready, now.n)
                    nc.scalar.activation(z01[:, :], psZ[:, :], ACT.Identity, bias=h.x01b_edge[:, :],
                                         scale=0.01).then_inc(z01_ready, 1)
                    turned_to(xnT[:, s, 0, :], now, 2)
                    turned_to(xnT[:, s, 1, :], now, 3)
                    for k in range(2):
                        act.wait_ge(yn_ready, 2 * now.n + 1 + k)
                        wait(act, lrn_ready, 2 * now.n - 1 + k)
                        nc.scalar.activation(y01[:, k, :], psY[k][:, :], ACT.Identity, bias=h.x01b_node[:, :],
                                             scale=0.01).then_inc(yn01_ready, 1)
                if g:
                    norm_scale(nc, act, h, g, a, b, var, lnv, rstd, var_ready, lnv_ready, rstd_ready, out_ready)
                g, a, b = t.group(0)
                if g:
                    wait(act, out_ready, g.n - 1)
                if last:
                    act.wait_ge(ee_ready, last.n + 1)
                    nc.scalar.activation(cen[:, g.slot, 2, :], psE[0][:, :], ACT.Copy).then_inc(ce_ready, 1)
                if now:
                    for k in range(2):
                        act.wait_ge(en_ready, 2 * now.n + 1 + k)
                        nc.scalar.activation(cen[:, g.slot, k, :], psE[k][:, :], ACT.Copy).then_inc(cn_ready, 1)

            run_steps(act, 2, step)

        @block.vector
        def _(dve):
            nc.vector.memset(erow[:, :, :], 0.0).then_inc(erow_zero, 1)

            def step(t):
                now, last, (g, a, b) = t.tile(0), t.tile(1), t.group(1)
                if last:
                    dve.wait_ge(ye01_ready, last.n + 1)
                    wait(dve, te_ready, last.n)
                    nc.vector.scalar_tensor_tensor(out=lr[:, 2, :], in0=psY[0][:, :], scalar=h.col("b_node"),
                                                   in1=y01[:, 2, :], op0=ALU.add, op1=ALU.max).then_inc(lre_ready, 1)
                if now:
                    s = now.slot
                    dve.wait_ge(z01_ready, now.n + 1)
                    wait(dve, red_ready, now.n)
                    nc.vector.scalar_tensor_tensor(out=msg[:, :], in0=psZ[:, :], scalar=h.col("b_edge"), in1=z01[:, :],
                                                   op0=ALU.add, op1=ALU.max).then_inc(msg_ready, 1)
                if last:
                    dve.wait_ge(lre_ready, last.n + 1)
                    wait(dve, ee_ready, last.n)
                    nc.vector.tensor_tensor(tT[:, 2, :], lr[:, 2, :], xdT[:, last.slot, :],
                                            ALU.add).then_inc(te_ready, 1)
                if now:
                    dve.wait_ge(msg_ready, now.n + 1)
                    wait(dve, ye_ready, now.n - 1)
                    first = 0.0 if isinstance(now.n, int) and now.n == 0 else red[:, 1 - s, TILE - 1:TILE]
                    wait(dve, red_ready, now.n)
                    nc.vector.tensor_tensor_scan(red[:, s, :], h.cont[:, bass.ds(now.n * TILE, TILE)], msg[:, :],
                                                 first, ALU.mult, ALU.add).then_inc(red_ready, 1)
                if g:
                    norm_sum(nc, dve, g, a, b, sq, var, sq_ready, var_ready, rstd_ready)
                if now:
                    for k in range(2):
                        dve.wait_ge(yn01_ready, 2 * now.n + 1 + k)
                        wait(dve, tn_ready, 2 * now.n - 1 + k)
                        nc.vector.scalar_tensor_tensor(out=lr[:, k, :], in0=psY[k][:, :], scalar=h.col("b_node"),
                                                       in1=y01[:, k, :], op0=ALU.add, op1=ALU.max).then_inc(lrn_ready, 1)
                    for k in range(2):
                        dve.wait_ge(lrn_ready, 2 * now.n + 1 + k)
                        wait(dve, en_ready, 2 * now.n - 1 + k)
                        nc.vector.tensor_tensor(tT[:, k, :], lr[:, k, :], xnT[:, s, k, :], ALU.add).then_inc(tn_ready, 1)
                if g:
                    norm_apply(nc, dve, t, g, a, b, cen, rstd, xo, rstd_ready, out_ready, node_stored, edge_stored)

            run_steps(dve, 2, step)


def gather_pair(nc, pool, h, now, table, ix, ix_ready, starts, xs, xd, src_landed, dst_landed, turned, per_step):
    s = now.slot
    wait(pool, src_landed[s], 64 * now.half)
    wait(pool, dst_landed[s], 64 * now.half)
    nc.gpsimd.tensor_copy(ix[:, s, 0:4], h.src_row[:, bass.ds(now.n * 4, 4)]).then_inc(ix_ready, 1)
    nc.gpsimd.tensor_copy(ix[:, s, 4:8], h.dst_row[:, bass.ds(now.n * 4, 4)]).then_inc(ix_ready, 1)
    wait(pool, turned, per_step * (now.n - 2) + 2)
    wait_for_dma(pool, ix_ready, 2 * now.n + 2, starts)
    for k, (rows, landed) in enumerate(((xs, src_landed), (xd, dst_landed))):
        for j in range(4):
            at = bass.IndirectOffsetOnAxis(ap=ix[:, s, 4 * k + j:4 * k + j + 1], axis=0)
            pool.indirect_dma_start(out=quarters(rows[:, s, :])[j], out_offset=None, in_=table,
                                    in_offset=at).then_inc(landed[s], 16)


def conv(nc, io, h, layer):
    with ExitStack() as ctx:
        ctx.enter_context(nc.cleanup_on_exit())
        tag = f"c{layer}_"
        sem = lambda name: nc.alloc_semaphore(tag + name)
        sb = lambda name, shape, dt=F32: ctx.enter_context(nc.sbuf_tensor(tag + name, shape, dt))
        bank = lambda name: ctx.enter_context(nc.psum_tensor(tag + name, [P, TILE], F32))
        table, result = (io["x1"], io["h1"]) if layer == 0 else (io["h1"], io["x2"])
        w_q, w_k, w_v = (h.w[f"{k}{layer}"] for k in "qkv")
        w_s = h.w["s0"] if layer == 0 else h.s1c
        to_rows = h.w["ident"] if layer == 0 else h.w["center"]
        s_bias = h.s_b0 if layer == 0 else h.s_b1c
        b_q, b_k, b_v = h.col(f"q_b{layer}"), h.col(f"k_b{layer}"), h.b_vs[:, layer:layer + 1]
        ix = sb("ix", [P, 2, 8], I32)
        xs, xd = sb("xs", [P, 2, TILE]), sb("xd", [P, 2, TILE])
        xsT, xdT = sb("xsT", [P, 2, TILE]), sb("xdT", [P, 2, TILE])
        xn, xnT = sb("xn", [P, 2, 2, TILE]), sb("xnT", [P, 2, 2, TILE])
        q, kq = sb("q", [P, TILE]), sb("kq", [P, TILE])
        m = sb("m", [P, 2, TILE + 1])
        drop, dropm, c, u, p = (sb(n, [P, TILE]) for n in ("drop", "dropm", "c", "u", "p"))
        pv, den, num = sb("pv", [P, TILE]), sb("den", [P, 2, TILE]), sb("num", [P, 2, TILE])
        lnd, rden, agg = (sb(n, [P, TILE]) for n in ("lnd", "rden", "agg"))
        pre, xo = sb("pre", [P, 2, 3, TILE]), sb("xo", [P, 2, 3, TILE])
        xe = None if layer else sb("xe", [P, 2, TILE])
        x1r = sb("x1r", [P, 2, 3, TILE]) if layer else None
        sq = sb("sq", [P, 3, TILE]) if layer else None
        var, lnv, rstd = sb("var", [P, 2, 12]), sb("lnv", [P, 12]), sb("rstd", [P, 2, 12])
        psT = [bank(f"psT{k}") for k in range(2)]
        psQ, psV, psA = bank("psQ"), bank("psV"), bank("psA")
        psE = [bank(f"psE{k}") for k in range(3)]
        src_landed, dst_landed, node_landed, x1n_landed, x1e_landed, node_stored, edge_stored = [
            [sem(f"{n}{s}") for s in range(2)] for n in
            ("src_landed", "dst_landed", "node_landed", "x1n_landed", "x1e_landed", "node_stored", "edge_stored")]
        (starts, starts_sp, ix_ready, turned, turned_sb, q_ready, q_sb, k_ready, v_ready, kq_ready, a_ready, carry_ready, m_ready,
         drop_ready, dropm_ready, c_ready, u_ready, p_ready, pv_ready, den_ready, num_ready, lnd_ready, rden_ready,
         agg_ready, en_ready, ee_ready, oute_ready, pren_ready, pree_ready, sq_ready, var_ready, lnv_ready, rstd_ready,
         out_ready) = map(sem, (
             "starts", "starts_sp", "ix_ready", "turned", "turned_sb", "q_ready", "q_sb", "k_ready", "v_ready", "kq_ready", "a_ready",
             "carry_ready", "m_ready", "drop_ready", "dropm_ready", "c_ready", "u_ready", "p_ready", "pv_ready",
             "den_ready", "num_ready", "lnd_ready", "rden_ready", "agg_ready", "en_ready", "ee_ready", "oute_ready",
             "pren_ready", "pree_ready", "sq_ready", "var_ready", "lnv_ready", "rstd_ready", "out_ready"))
        block = ctx.enter_context(nc.Block())

        @block.gpsimd
        def _(pool):
            def step(t):
                now = t.tile(0)
                gather_pair(nc, pool, h, now, table, ix, ix_ready, starts, xs, xd, src_landed, dst_landed, turned, 4)

            run_steps(pool, 0, step)

        @block.sync
        def _(sp):
            def step(t):
                now, last, (g, a, b) = t.tile(0), t.tile(1), t.group(2)
                if now:
                    s = now.slot
                    wait(sp, turned, 4 * now.n - 4)
                    sp.dma_start(xn[:, s, :, :], node_rows(table, now.n)).then_inc(node_landed[s], 16)
                if layer:
                    u0 = t.group(0)[0]
                    if u0:
                        wait(sp, pren_ready, 2 * u0.n - 2)
                        sp.sem_inc(starts_sp, 1)
                        wait(sp, pree_ready, u0.n - 2)
                        sp.sem_inc(starts_sp, 1)
                    if now:
                        sp.dma_start(x1r[:, u0.slot, 0:2, :], node_rows(io["x1"], now.n)).then_inc(x1n_landed[now.slot], 16)
                    if last:
                        sp.dma_start(by_row(x1r[:, u0.slot, 2, :]),
                                     edge_rows(io["x1"], last.n)).then_inc(x1e_landed[last.slot], 16)
                if layer:
                    store_group(sp, g, a, b, t, result, xo, out_ready, node_stored, edge_stored)
                    return
                if last:
                    sp.wait_ge(out_ready, last.n + 1)
                    sp.dma_start(node_rows(result, last.n), xo[:, last.slot, 0:2, :]).then_inc(node_stored[last.slot], 16)
                old = t.tile(3)
                if old:
                    sp.wait_ge(oute_ready, old.n + 1)
                    sp.dma_start(edge_rows(result, old.n), by_row(xe[:, old.slot, :])).then_inc(edge_stored[old.slot], 16)

            run_steps(sp, 3, step)
            all_stored(sp, node_stored, edge_stored)

        @block.tensor
        def _(pe):
            def turn(k, now, rows, landed, count):
                pe.wait_ge(landed, count)
                wait(pe, turned_sb, 4 * now.n + k - 1)
                for o, x in zip(quarters(psT[k % 2]), quarters(rows)):
                    ins = nc.tensor.transpose(o, x, h.w["ident"][:, :])
                ins.then_inc(turned, 1)

            def own_rows(now, k):
                pe.wait_ge(turned_sb, 4 * now.n + 3 + k)
                wait(pe, pren_ready, 2 * now.n - 1 + k)
                for o, x in zip(quarters(psE[k]), quarters(xnT[:, now.slot, k, :])):
                    ins = nc.tensor.matmul(o, x, w_s[:, :], start=True, stop=not layer)
                    if layer:
                        ins = nc.tensor.matmul(o, h.avg[:, :], s_bias[:, :], start=False, stop=True)
                ins.then_inc(en_ready, 1)

            def step(t):
                now, last = t.tile(0), t.tile(1)
                if now:
                    s = now.slot
                    turn(0, now, xs[:, s, :], src_landed[s], 64 * (now.half + 1))
                    turn(1, now, xd[:, s, :], dst_landed[s], 64 * (now.half + 1))
                    pe.wait_ge(turned_sb, 4 * now.n + 2)
                    wait(pe, kq_ready, now.n)
                    nc.tensor.matmul(psQ[:, :], w_q[:, :], xdT[:, s, :], start=True, stop=True).then_inc(q_ready, 1)
                    turn(2, now, xn[:, s, 0, :], node_landed[s], 16 * (now.half + 1))
                    turn(3, now, xn[:, s, 1, :], node_landed[s], 16 * (now.half + 1))
                    pe.wait_ge(q_sb, now.n + 1)
                    nc.tensor.matmul(psQ[:, :], w_k[:, :], xsT[:, s, :], start=True, stop=True).then_inc(k_ready, 1)
                    wait(pe, pv_ready, now.n)
                    nc.tensor.matmul(psV[:, :], w_v[:, :], xsT[:, s, :], start=True, stop=True).then_inc(v_ready, 1)
                    own_rows(now, 0)
                    pe.wait_ge(kq_ready, now.n + 1)
                    wait(pe, u_ready, now.n)
                    nc.tensor.matmul(psA[:, :], h.w["heads8"][:, :], kq[:, :], start=True, stop=True).then_inc(a_ready, 1)
                    own_rows(now, 1)
                if last:
                    pe.wait_ge(agg_ready, last.n + 1)
                    wait(pe, pree_ready if layer else oute_ready, last.n)
                    for o, x, y in zip(quarters(psE[2]), quarters(agg), quarters(xdT[:, last.slot, :])):
                        nc.tensor.matmul(o, x, to_rows[:, :], start=True, stop=False)
                        ins = nc.tensor.matmul(o, y, w_s[:, :], start=False, stop=True)
                    ins.then_inc(ee_ready, 1)

            run_steps(pe, 1, step)

        @block.scalar
        def _(act):
            nc.scalar.preload_act_table_set(LN_EXP)

            def step(t):
                now, last, old, (g, a, b) = t.tile(0), t.tile(1), t.tile(2), t.group(1)
                if now:
                    s = now.slot
                    for k, dst in enumerate((xsT[:, s, :], xdT[:, s, :])):
                        act.wait_ge(turned, 4 * now.n + k + 1)
                        if k == 0:
                            wait(act, v_ready, now.n - 1)
                        else:
                            wait(act, ee_ready, now.n - 1)
                        nc.scalar.activation(dst, psT[k][:, :], ACT.Copy).then_inc(turned_sb, 1)
                if layer and g:
                    if a == 0:
                        act.wait_ge(pren_ready, 2 * g.n + 2)
                    if b == 3:
                        act.wait_ge(pree_ready, g.n)
                    wait(act, var_ready, g.n)
                    nc.scalar.activation(sq[:, a:b, :], pre[:, g.slot, a:b, :], ACT.Square).then_inc(sq_ready, 1)
                if last:
                    act.wait_ge(dropm_ready, last.n + 1)
                    wait(act, num_ready, last.n)
                    nc.scalar.activation(c[:, :], dropm[:, :], ACT.Exp).then_inc(c_ready, 1)
                    act.wait_ge(u_ready, last.n + 1)
                    wait(act, pv_ready, last.n)
                    wait(act, den_ready, last.n)
                    nc.scalar.activation(p[:, :], u[:, :], ACT.Exp).then_inc(p_ready, 1)
                if old and not layer:
                    act.wait_ge(ee_ready, old.n + 1)
                    wait(act, edge_stored[old.slot], 16 * old.half)
                    nc.scalar.activation(xe[:, old.slot, :], psE[2][:, :], ACT.Relu).then_inc(oute_ready, 1)
                if now:
                    act.wait_ge(q_ready, now.n + 1)
                    wait(act, kq_ready, now.n)
                    nc.scalar.activation(q[:, :], psQ[:, :], ACT.Identity, bias=b_q).then_inc(q_sb, 1)
                    for k in range(2):
                        act.wait_ge(turned, 4 * now.n + k + 3)
                        wait(act, en_ready, 2 * now.n - 3 + k)
                        nc.scalar.activation(xnT[:, s, k, :], psT[k][:, :], ACT.Copy).then_inc(turned_sb, 1)
                if layer and g:
                    norm_scale(nc, act, h, g, a, b, var, lnv, rstd, var_ready, lnv_ready, rstd_ready, out_ready)
                if last:
                    act.wait_ge(den_ready, last.n + 1)
                    wait(act, rden_ready, last.n)
                    nc.scalar.activation(lnd[:, :], den[:, last.slot, :], ACT.Ln).then_inc(lnd_ready, 1)
                    act.wait_ge(lnd_ready, last.n + 1)
                    wait(act, agg_ready, last.n)
                    nc.scalar.activation(rden[:, :], lnd[:, :], ACT.Exp, scale=-1.0).then_inc(rden_ready, 1)
                if layer and g:
                    act.wait_ge(rstd_ready, g.n + 1)
                    free_of_stores(act, t, g, a, b, node_stored, edge_stored)
                    for j in range(4 * a, 4 * b):
                        ins = nc.scalar.activation(quarters(xo[:, g.slot, j // 4, :])[j % 4],
                                                   quarters(pre[:, g.slot, j // 4, :])[j % 4], ACT.Copy,
                                                   scale=rstd[:, g.slot, j:j + 1])
                    ins.then_inc(out_ready, 1)
                if now and not layer:
                    act.wait_ge(pren_ready, 2 * now.n + 2)
                    wait(act, node_stored[s], 16 * now.half)
                    nc.scalar.activation(xo[:, s, 0:2, :], pre[:, s, 0:2, :], ACT.Relu).then_inc(out_ready, 1)

            run_steps(act, 2, step)

        @block.vector
        def _(dve):
            nc.vector.memset(m[:, 0, 0:1], 0.0).then_inc(carry_ready, 1)

            def add_x1(t, g, k):
                now, last = t.tile(0), t.tile(1)
                if k < 2:
                    dve.wait_ge(en_ready, 2 * now.n + 1 + k)
                    dve.wait_ge(x1n_landed[now.slot], 16 * (now.half + 1))
                else:
                    dve.wait_ge(ee_ready, last.n + 1)
                    dve.wait_ge(x1e_landed[last.slot], 16 * (last.half + 1))
                nc.vector.tensor_tensor(pre[:, g.slot, k, :], psE[k][:, :], x1r[:, g.slot, k, :],
                                        ALU.add).then_inc(pren_ready if k < 2 else pree_ready, 1)

            def step(t):
                now, last, (g, a, b) = t.tile(0), t.tile(1), t.group(1)
                if last:
                    s = last.slot
                    dve.wait_ge(a_ready, last.n + 1)
                    dve.wait_ge(carry_ready, last.n + 1)
                    here = bass.ds(last.n * TILE, TILE)
                    nc.vector.tensor_tensor_scan(m[:, s, 1:TILE + 1], h.far[:, here], psA[:, :], m[:, s, 0:1],
                                                 ALU.add, ALU.max).then_inc(m_ready, 1)
                    dve.wait_ge(m_ready, last.n + 1)
                    wait(dve, dropm_ready, last.n)
                    nc.vector.tensor_tensor(drop[:, :], m[:, s, 0:TILE], m[:, s, 1:TILE + 1],
                                            ALU.subtract).then_inc(drop_ready, 1)
                    wait(dve, p_ready, last.n)
                    nc.vector.tensor_tensor(u[:, :], psA[:, :], m[:, s, 1:TILE + 1], ALU.subtract).then_inc(u_ready, 1)
                    dve.wait_ge(drop_ready, last.n + 1)
                    wait(dve, c_ready, last.n)
                    nc.vector.scalar_tensor_tensor(out=dropm[:, :], in0=drop[:, :], scalar=0.0, in1=h.far[:, here],
                                                   op0=ALU.min, op1=ALU.add).then_inc(dropm_ready, 1)
                    wait(dve, drop_ready, last.n)
                    nc.vector.tensor_copy(m[:, 1 - s, 0:1], m[:, s, TILE:TILE + 1]).then_inc(carry_ready, 1)
                if layer and g:
                    norm_sum(nc, dve, g, a, b, sq, var, sq_ready, var_ready, rstd_ready)
                if last:
                    dve.wait_ge(p_ready, last.n + 1)
                    wait(dve, num_ready, last.n)
                    nc.vector.scalar_tensor_tensor(out=pv[:, :], in0=psV[:, :], scalar=b_v, in1=p[:, :],
                                                   op0=ALU.add, op1=ALU.mult).then_inc(pv_ready, 1)
                    first = isinstance(last.n, int) and last.n == 0
                    dve.wait_ge(c_ready, last.n + 1)
                    wait(dve, lnd_ready, last.n - 1)
                    wait(dve, den_ready, last.n)
                    nc.vector.tensor_tensor_scan(den[:, s, :], c[:, :], p[:, :],
                                                 0.0 if first else den[:, 1 - s, TILE - 1:TILE],
                                                 ALU.mult, ALU.add).then_inc(den_ready, 1)
                    dve.wait_ge(pv_ready, last.n + 1)
                    wait(dve, agg_ready, last.n - 1)
                    wait(dve, num_ready, last.n)
                    nc.vector.tensor_tensor_scan(num[:, s, :], c[:, :], pv[:, :],
                                                 0.0 if first else num[:, 1 - s, TILE - 1:TILE],
                                                 ALU.mult, ALU.add).then_inc(num_ready, 1)
                if now:
                    dve.wait_ge(k_ready, now.n + 1)
                    dve.wait_ge(q_sb, now.n + 1)
                    wait(dve, a_ready, now.n)
                    nc.vector.scalar_tensor_tensor(out=kq[:, :], in0=psQ[:, :], scalar=b_k, in1=q[:, :],
                                                   op0=ALU.add, op1=ALU.mult).then_inc(kq_ready, 1)
                if last:
                    dve.wait_ge(rden_ready, last.n + 1)
                    dve.wait_ge(num_ready, last.n + 1)
                    wait(dve, ee_ready, last.n)
                    nc.vector.tensor_tensor(agg[:, :], num[:, last.slot, :], rden[:, :], ALU.mult).then_inc(agg_ready, 1)
                if now and not layer:
                    wait(dve, out_ready, now.n - 1)
                    for k in range(2):
                        dve.wait_ge(en_ready, 2 * now.n + 1 + k)
                        nc.vector.tensor_tensor(by_row(pre[:, now.slot, k, :]), by_row(psE[k][:, :]),
                                                s_bias[:, :].rearrange("p (o f) -> p o f", o=1).to_broadcast([P, 4, P]),
                                                ALU.add).then_inc(pren_ready, 1)
                if layer:
                    g0, a0, b0 = t.group(0)
                    if g0:
                        wait(dve, out_ready, g0.n - 1)
                    for k in range(a0, b0):
                        add_x1(t, g0, k)

            run_steps(dve, 2 if layer else 1, step)


def layer2(nc, io, h):
    with ExitStack() as ctx:
        ctx.enter_context(nc.cleanup_on_exit())
        sem = lambda name: nc.alloc_semaphore("g_" + name)
        sb = lambda name, shape, dt=F32: ctx.enter_context(nc.sbuf_tensor("g_" + name, shape, dt))
        bank = lambda name: ctx.enter_context(nc.psum_tensor("g_" + name, [P, TILE], F32))
        table = io["x2"]
        ix = sb("ix", [P, 2, 8], I32)
        xs, xd = sb("xs", [P, 2, TILE]), sb("xd", [P, 2, TILE])
        xsT, xdT = sb("xsT", [P, 2, TILE]), sb("xdT", [P, 2, TILE])
        xn, xnT = sb("xn", [P, 2, 2, TILE]), sb("xnT", [P, 2, 2, TILE])
        erow = sb("erow", [P, 2, TILE])
        far = sb("far", [P, 2, TILE], BF16)
        z02, zs02, zl, zsl, lself, top = (sb(n, [P, TILE]) for n in ("z02", "zs02", "zl", "zsl", "lself", "top"))
        m = sb("m", [P, 2, TILE + 1])
        drop, dropm, c, u, us, p, ps = (sb(n, [P, TILE]) for n in ("drop", "dropm", "c", "u", "us", "p", "ps"))
        both, pv, pvs = (sb(n, [P, TILE]) for n in ("both", "pv", "pvs"))
        den, num = sb("den", [P, 2, TILE]), sb("num", [P, 2, TILE])
        rden, agg = sb("rden", [P, TILE]), sb("agg", [P, TILE])
        gT, x2r = sb("gT", [P, 3, TILE]), sb("x2r", [P, 2, 3, TILE])
        pre1, n1, affT, pre2 = (sb(n, [P, 3, TILE]) for n in ("pre1", "n1", "affT", "pre2"))
        x3o, x4o = sb("x3o", [P, 2, 3, TILE]), sb("x4o", [P, 2, 2, TILE])
        sq1, sq2, sq3 = sb("sq1", [P, 3, TILE]), sb("sq2", [P, 3, TILE]), sb("sq3", [P, 2, TILE])
        var, lnv, rstd = ([sb(f"{n}{k}", [P, 12]) for k in range(3)] for n in ("var", "lnv", "rstd"))
        psT = [bank(f"psT{k}") for k in range(2)]
        psZ, psY, psV, psS, psA, psE = (bank(n) for n in ("psZ", "psY", "psV", "psS", "psA", "psE"))
        psF, psG = (psE, psT[1], psT[0]), (psT[1], psT[0], psE)
        (src_landed, dst_landed, node_landed, erow_landed, far_landed, x2n_landed, x2e_landed, node_stored,
         edge_stored, out_stored) = [[sem(f"{n}{s}") for s in range(2)] for n in (
             "src_landed", "dst_landed", "node_landed", "erow_landed", "far_landed", "x2n_landed", "x2e_landed",
             "node_stored", "edge_stored", "out_stored")]
        (starts, starts_sp, ix_ready, turned, turned_sb, erow_zero, z_ready, zs_ready, z02_ready, zs02_ready, zl_ready, zsl_ready,
         y_ready, v_ready, s_ready, a_ready, as_ready, lself_ready, top_ready, carry_ready, m_ready, drop_ready,
         dropm_ready, u_ready, us_ready, c_ready, p_ready, ps_ready, both_ready, pv_ready, pvs_ready, ptot_ready,
         den_ready, num_ready, lnd_ready, rden_ready, agg_ready, gn_ready, ge_ready, en_ready, ee_ready, pre1n_ready,
         pre1e_ready, n1_ready, n1n_turned, n1e_turned, affn_ready, affe_ready, fn_ready, fe_ready, pre2n_ready,
         pre2e_ready, x3_ready, x4_ready) = map(sem, (
             "starts", "starts_sp", "ix_ready", "turned", "turned_sb", "erow_zero", "z_ready", "zs_ready", "z02_ready",
             "zs02_ready", "zl_ready", "zsl_ready", "y_ready", "v_ready", "s_ready", "a_ready", "as_ready",
             "lself_ready", "top_ready", "carry_ready", "m_ready", "drop_ready", "dropm_ready", "u_ready", "us_ready",
             "c_ready", "p_ready", "ps_ready", "both_ready", "pv_ready", "pvs_ready", "ptot_ready", "den_ready",
             "num_ready", "lnd_ready", "rden_ready", "agg_ready", "gn_ready", "ge_ready", "en_ready", "ee_ready",
             "pre1n_ready", "pre1e_ready", "n1_ready", "n1n_turned", "n1e_turned", "affn_ready", "affe_ready",
             "fn_ready", "fe_ready", "pre2n_ready", "pre2e_ready", "x3_ready", "x4_ready"))
        sq_ready, var_ready, lnv_ready, rstd_ready = ([sem(f"{n}{k}") for k in range(3)] for n in (
            "sq_ready", "var_ready", "lnv_ready", "rstd_ready"))
        block = ctx.enter_context(nc.Block())

        @block.gpsimd
        def _(pool):
            def step(t):
                now, old, (g, a, _) = t.tile(0), t.tile(2), t.group(4)
                if now:
                    gather_pair(nc, pool, h, now, table, ix, ix_ready, starts, xs, xd, src_landed, dst_landed,
                                turned, 4)
                if old:
                    pool.wait_ge(m_ready, old.n + 1)
                    pool.wait_ge(lself_ready, old.n + 1)
                    wait(pool, ps_ready, old.n)
                    nc.gpsimd.tensor_tensor(us[:, :], lself[:, :], m[:, old.slot, 1:TILE + 1],
                                            ALU.subtract).then_inc(us_ready, 1)
                    pool.wait_ge(ps_ready, old.n + 1)
                    pool.wait_ge(p_ready, old.n + 1)
                    wait(pool, den_ready, old.n)
                    nc.gpsimd.tensor_tensor(both[:, :], p[:, :], ps[:, :], ALU.add).then_inc(both_ready, 1)
                if g and a == 0:
                    pool.wait_ge(rstd_ready[2], g.n + 1)
                    pool.wait_ge(x3_ready, g.n + 1)
                    wait(pool, out_stored[g.slot], 16 * g.half)
                    nc.gpsimd.tensor_tensor(by_row(x4o[:, g.slot, :, :].rearrange("p b n -> p (b n)")),
                                            by_row(x3o[:, g.slot, 0:2, :].rearrange("p b n -> p (b n)")),
                                            rstd[2][:, 0:8].rearrange("p (b o) -> p b o", o=1).to_broadcast([P, 8, P]),
                                            ALU.mult).then_inc(x4_ready, 1)

            run_steps(pool, 4, step)

        @block.sync
        def _(sp):
            sp.wait_ge(erow_zero, 1)

            def step(t):
                now, last, (g0, _, _), (g2, a2, b2), (g3, a3, b3) = (
                    t.tile(0), t.tile(1), t.group(0), t.group(3), t.group(4))
                if now:
                    s = now.slot
                    wait(sp, turned, 4 * now.n - 4)
                    sp.dma_start(xn[:, s, :, :], node_rows(table, now.n)).then_inc(node_landed[s], 16)
                    wait(sp, z_ready, now.n - 1)
                    sp.dma_start(erow[0:1, s, :],
                                 io["ew1"][:, bass.ds(now.n * TILE, TILE)]).then_inc(erow_landed[s], 16)
                    wait(sp, dropm_ready, now.n - 1)
                    sp.sem_inc(starts_sp, 1)
                    sp.dma_start(far[:, s, :], io["far"][:, bass.ds(now.n * TILE, TILE)].to_broadcast([P, TILE])
                                 ).then_inc(far_landed[s], 16)
                if g0:
                    wait(sp, pre2n_ready, 2 * g0.n - 2)
                    sp.sem_inc(starts_sp, 1)
                    wait(sp, pre2e_ready, g0.n - 2)
                    sp.sem_inc(starts_sp, 1)
                    if now:
                        sp.dma_start(x2r[:, g0.slot, 0:2, :], node_rows(table, now.n)).then_inc(x2n_landed[now.slot], 16)
                    if last:
                        sp.dma_start(by_row(x2r[:, g0.slot, 2, :]),
                                     edge_rows(table, last.n)).then_inc(x2e_landed[last.slot], 16)
                store_group(sp, g2, a2, b2, t, io["x3"], x3o, x3_ready, node_stored, edge_stored)
                if g3 and a3 == 0:
                    sp.wait_ge(x4_ready, g3.n + 1)
                    sp.dma_start(node_rows(io["out"], g3.n), x4o[:, g3.slot, :, :]).then_inc(out_stored[g3.slot], 16)

            run_steps(sp, 4, step)
            all_stored(sp, node_stored, edge_stored)
            for s in range(2):
                sp.wait_ge(out_stored[s], 16 * STEPS // 2)

        @block.tensor
        def _(pe):
            def turned_rows(dst, src):
                for o, x in zip(quarters(dst), quarters(src)):
                    ins = nc.tensor.transpose(o, x, h.w["ident"][:, :])
                return ins

            def centred(dst, src):
                for o, x in zip(quarters(dst), quarters(src)):
                    ins = nc.tensor.matmul(o, x, h.w["center"][:, :], start=True, stop=True)
                return ins

            def step(t):
                now, last, (g, a, b) = t.tile(0), t.tile(1), t.group(1)
                before, _, before_b = t.group(2)
                if now:
                    s = now.slot
                    for k, (rows, landed) in enumerate(((xs, src_landed), (xd, dst_landed))):
                        pe.wait_ge(landed[s], 64 * (now.half + 1))
                        wait(pe, pre1n_ready, 2 * now.n - k)
                        turned_rows(psT[k], rows[:, s, :]).then_inc(turned, 1)
                    pe.wait_ge(turned_sb, 4 * now.n + 2)
                    pe.wait_ge(erow_landed[s], 16 * (now.half + 1))
                    wait(pe, gn_ready, 2 * now.n - 1)
                    nc.tensor.matmul(psZ[:, :], h.w["w_l"][:, :], xsT[:, s, :], start=True, stop=False)
                    nc.tensor.matmul(psZ[:, :], h.w["w_r"][:, :], xdT[:, s, :], start=False, stop=False)
                    nc.tensor.matmul(psZ[:, :], h.w_e_row[:, :], erow[:, s, :],
                                     start=False, stop=True).then_inc(z_ready, 1)
                    wait(pe, gn_ready, 2 * now.n)
                    nc.tensor.matmul(psY[:, :], h.w_lr[:, :], xdT[:, s, :], start=True, stop=True).then_inc(zs_ready, 1)
                    pe.wait_ge(node_landed[s], 16 * (now.half + 1))
                    for k in range(2):
                        turned_rows(psT[k], xn[:, s, k, :]).then_inc(turned, 1)
                    pe.wait_ge(zsl_ready, now.n + 1)
                    wait(pe, u_ready, now.n)
                    nc.tensor.matmul(psA[:, :], h.att_m[:, :], zsl[:, :], start=True, stop=True).then_inc(as_ready, 1)
                    for k, (ps_, read) in enumerate(((psZ, zl_ready), (psY, zsl_ready))):
                        pe.wait_ge(turned_sb, 4 * now.n + 3 + k)
                        pe.wait_ge(read, now.n + 1)
                        nc.tensor.matmul(ps_[:, :], h.w["w_l"][:, :], xnT[:, s, k, :],
                                         start=True, stop=True).then_inc(y_ready, 1)
                    pe.wait_ge(lself_ready, now.n + 1)
                    nc.tensor.matmul(psA[:, :], h.att_m[:, :], zl[:, :], start=True, stop=True).then_inc(a_ready, 1)
                if g:
                    pe.wait_ge(n1_ready, g.n + 1)
                    for k in range(a, min(b, 2)):
                        if now:
                            pe.wait_ge(turned_sb, 4 * now.n + 3 + k)
                        turned_rows(psT[k], n1[:, k, :]).then_inc(n1n_turned, 1)
                if now:
                    wait(pe, pv_ready, now.n)
                    nc.tensor.matmul(psV[:, :], h.w["w_l"][:, :], xsT[:, s, :], start=True, stop=True).then_inc(v_ready, 1)
                if g and b == 3:
                    if a == 0:
                        pe.wait_ge(affn_ready, 2 * g.n + 1)
                    turned_rows(psT[0], n1[:, 2, :]).then_inc(n1e_turned, 1)
                if now:
                    wait(pe, pvs_ready, now.n)
                    nc.tensor.matmul(psS[:, :], h.w["w_l"][:, :], xdT[:, s, :], start=True, stop=True).then_inc(s_ready, 1)
                if g:
                    for k in range(a, b):
                        if k == 2:
                            pe.wait_ge(affe_ready, g.n)
                            centred(psF[2], affT[:, 2, :]).then_inc(fe_ready, 1)
                        else:
                            pe.wait_ge(affn_ready, 2 * g.n + 1 + k)
                            if k == 0:
                                wait(pe, pre1e_ready, g.n)
                            centred(psF[k], affT[:, k, :]).then_inc(fn_ready, 1)
                if now:
                    for k in range(2):
                        pe.wait_ge(gn_ready, 2 * now.n + 1 + k)
                        if k == 0:
                            wait(pe, pre2n_ready, 2 * now.n)
                        else:
                            wait(pe, pre2e_ready, now.n - 1)
                        centred(psG[k], gT[:, k, :]).then_inc(en_ready, 1)
                if last:
                    pe.wait_ge(ge_ready, last.n + 1)
                    pe.wait_ge(pre2n_ready, 2 * g.n + 1)
                    centred(psG[2], gT[:, 2, :]).then_inc(ee_ready, 1)

            run_steps(pe, 2, step)

        @block.scalar
        def _(act):
            nc.scalar.preload_act_table_set(LN_EXP)

            def step(t):
                now, last = t.tile(0), t.tile(1)
                (g1, a1, b1), (g2, a2, b2), (g3, a3, b3) = (t.group(k) for k in (1, 2, 3))
                if now:
                    s = now.slot
                    for k, dst in enumerate((xsT[:, s, :], xdT[:, s, :])):
                        act.wait_ge(turned, 4 * now.n + k + 1)
                        wait(act, v_ready if k == 0 else s_ready, now.n - 1)
                        nc.scalar.activation(dst, psT[k][:, :], ACT.Copy).then_inc(turned_sb, 1)
                if g1:
                    if a1 == 0:
                        act.wait_ge(pre1n_ready, 2 * g1.n + 2)
                    if b1 == 3:
                        act.wait_ge(pre1e_ready, g1.n)
                    wait(act, var_ready[0], g1.n)
                    nc.scalar.activation(sq1[:, a1:b1, :], pre1[:, a1:b1, :], ACT.Square).then_inc(sq_ready[0], 1)
                if now:
                    for ps_, ready, count_ready, bias, dst, read in (
                            (psZ, z_ready, z02_ready, h.x2blr, z02, zl_ready),
                            (psY, zs_ready, zs02_ready, h.x2b_self, zs02, zsl_ready)):
                        act.wait_ge(ready, now.n + 1)
                        wait(act, read, now.n)
                        nc.scalar.activation(dst[:, :], ps_[:, :], ACT.Identity, bias=bias[:, :],
                                             scale=0.2).then_inc(count_ready, 1)
                nc.scalar.preload_act_table_set(LN_EXP)
                if last:
                    act.wait_ge(dropm_ready, last.n + 1)
                    wait(act, num_ready, last.n)
                    nc.scalar.activation(c[:, :], dropm[:, :], ACT.Exp).then_inc(c_ready, 1)
                    act.wait_ge(u_ready, last.n + 1)
                    wait(act, pv_ready, last.n)
                    wait(act, both_ready, last.n)
                    nc.scalar.activation(p[:, :], u[:, :], ACT.Exp).then_inc(p_ready, 1)
                    act.wait_ge(us_ready, last.n + 1)
                    wait(act, pvs_ready, last.n)
                    nc.scalar.activation(ps[:, :], us[:, :], ACT.Exp).then_inc(ps_ready, 1)
                if now:
                    for k in range(2):
                        act.wait_ge(turned, 4 * now.n + k + 3)
                        wait(act, y_ready, 2 * now.n - 3 + k)
                        nc.scalar.activation(xnT[:, s, k, :], psT[k][:, :], ACT.Copy).then_inc(turned_sb, 1)
                for k, g, a, b, used, eps in ((0, g1, a1, b1, n1_ready, h.eps), (1, g2, a2, b2, x3_ready, h.eps),
                                              (2, g3, a3, min(b3, 2), x4_ready, h.eps4)):
                    if g and a < b:
                        act.wait_ge(var_ready[k], g.n + 1)
                        wait(act, rstd_ready[k], g.n)
                        nc.scalar.activation(lnv[k][:, 4 * a:4 * b], var[k][:, 4 * a:4 * b], ACT.Ln,
                                             bias=eps[:, :], scale=1.0 / P).then_inc(lnv_ready[k], 1)
                        act.wait_ge(lnv_ready[k], g.n + 1)
                        wait(act, used, g.n)
                        nc.scalar.activation(rstd[k][:, 4 * a:4 * b], lnv[k][:, 4 * a:4 * b], ACT.Exp,
                                             scale=-0.5).then_inc(rstd_ready[k], 1)
                if g2:
                    free_of_stores(act, t, g2, a2, b2, node_stored, edge_stored)
                    wait(act, x4_ready, g2.n - 1)
                    act.wait_ge(rstd_ready[1], g2.n + 1)
                    for j in range(4 * a2, 4 * b2):
                        ins = nc.scalar.activation(quarters(x3o[:, g2.slot, j // 4, :])[j % 4],
                                                   quarters(pre2[:, j // 4, :])[j % 4], ACT.Copy,
                                                   scale=rstd[1][:, j:j + 1])
                    ins.then_inc(x3_ready, 1)
                if g1:
                    for k in range(a1, b1):
                        if k == 2:
                            act.wait_ge(n1e_turned, g1.n)
                            wait(act, fe_ready, g1.n - 1)
                        else:
                            act.wait_ge(n1n_turned, 2 * g1.n + 1 + k)
                            wait(act, fn_ready, 2 * g1.n - 1 + k)
                        nc.scalar.activation(affT[:, k, :], psT[k % 2][:, :], ACT.Identity, bias=h.col("ln_b"),
                                             scale=h.col("ln_w")).then_inc(affe_ready if k == 2 else affn_ready, 1)
                if last:
                    act.wait_ge(den_ready, last.n + 1)
                    wait(act, agg_ready, last.n)
                    nc.scalar.activation(rden[:, :], den[:, last.slot, :], ACT.Ln,
                                         bias=h.den_eps[:, :]).then_inc(lnd_ready, 1)
                    act.wait_ge(lnd_ready, last.n + 1)
                    nc.scalar.activation(rden[:, :], rden[:, :], ACT.Exp, scale=-1.0).then_inc(rden_ready, 1)
                if now:
                    for k, ps_ in enumerate((psZ, psY)):
                        act.wait_ge(y_ready, 2 * now.n + 1 + k)
                        wait(act, en_ready, 2 * now.n - 1 + k)
                        nc.scalar.activation(gT[:, k, :], ps_[:, :], ACT.Gelu, bias=h.bl_out[:, :],
                                             scale=1.0 / (1.0 + DEN_EPS)).then_inc(gn_ready, 1)
                if last:
                    act.wait_ge(agg_ready, last.n + 1)
                    wait(act, ee_ready, last.n)
                    nc.scalar.activation(gT[:, 2, :], agg[:, :], ACT.Gelu, bias=h.col("g_bias")).then_inc(ge_ready, 1)
                if g2 and a2 == 0:
                    act.wait_ge(x3_ready, g2.n + 1)
                    wait(act, var_ready[2], g2.n)
                    nc.scalar.activation(sq3[:, :, :], x3o[:, g2.slot, 0:2, :], ACT.Square).then_inc(sq_ready[2], 1)
                if g1:
                    if a1 == 0:
                        act.wait_ge(pre2n_ready, 2 * g1.n + 2)
                    if b1 == 3:
                        act.wait_ge(pre2e_ready, g1.n)
                    wait(act, var_ready[1], g1.n)
                    nc.scalar.activation(sq2[:, a1:b1, :], pre2[:, a1:b1, :], ACT.Square).then_inc(sq_ready[1], 1)

            run_steps(act, 3, step)

        @block.vector
        def _(dve):
            def sums(k, g, a, b, sq):
                if g and a < b:
                    dve.wait_ge(sq_ready[k], g.n + 1)
                    wait(dve, rstd_ready[k], g.n)
                    nc.vector.tensor_reduce(var[k][:, 4 * a:4 * b], by_row(sq[:, a:b, :].rearrange(
                        "p b n -> p (b n)")), AX_X, ALU.add).then_inc(var_ready[k], 1)

            nc.vector.memset(erow[:, :, :], 0.0).then_inc(erow_zero, 1)
            nc.vector.memset(m[:, 0, 0:1], 0.0).then_inc(carry_ready, 1)

            def scaled(k, g, dst, src, a, b, ready):
                dve.wait_ge(rstd_ready[k], g.n + 1)
                scale = rstd[k][:, 4 * a:4 * b].rearrange("p (b o) -> p b o", o=1).to_broadcast([P, 4 * (b - a), P])
                nc.vector.tensor_tensor(by_row(dst.rearrange("p b n -> p (b n)")),
                                        by_row(src.rearrange("p b n -> p (b n)")), scale, ALU.mult).then_inc(ready, 1)

            def step(t):
                now, last = t.tile(0), t.tile(1)
                (g0, a0, b0), (g1, a1, b1), (g2, a2, b2), (g3, a3, b3) = (t.group(k) for k in range(4))
                if last:
                    s = last.slot
                    dve.wait_ge(a_ready, last.n + 1)
                    dve.wait_ge(lself_ready, last.n + 1)
                    wait(dve, m_ready, last.n)
                    nc.vector.tensor_tensor(top[:, :], psA[:, :], lself[:, :], ALU.max).then_inc(top_ready, 1)
                    dve.wait_ge(top_ready, last.n + 1)
                    dve.wait_ge(carry_ready, last.n + 1)
                    nc.vector.tensor_tensor_scan(m[:, s, 1:TILE + 1], far[:, s, :], top[:, :], m[:, s, 0:1],
                                                 ALU.add, ALU.max).then_inc(m_ready, 1)
                    dve.wait_ge(m_ready, last.n + 1)
                    wait(dve, dropm_ready, last.n)
                    nc.vector.tensor_tensor(drop[:, :], m[:, s, 0:TILE], m[:, s, 1:TILE + 1],
                                            ALU.subtract).then_inc(drop_ready, 1)
                    wait(dve, p_ready, last.n)
                    nc.vector.tensor_tensor(u[:, :], psA[:, :], m[:, s, 1:TILE + 1], ALU.subtract).then_inc(u_ready, 1)
                    dve.wait_ge(drop_ready, last.n + 1)
                    wait(dve, c_ready, last.n)
                    nc.vector.scalar_tensor_tensor(out=dropm[:, :], in0=drop[:, :], scalar=0.0, in1=far[:, s, :],
                                                   op0=ALU.min, op1=ALU.add).then_inc(dropm_ready, 1)
                    nc.vector.tensor_copy(m[:, 1 - s, 0:1], m[:, s, TILE:TILE + 1]).then_inc(carry_ready, 1)
                sums(0, g1, a1, b1, sq1)
                sums(1, g2, a2, b2, sq2)
                if now:
                    for ps_, ready, bias, low, dst, done, used in (
                            (psY, zs02_ready, h.b_self, zs02, zsl, zsl_ready, as_ready),
                            (psZ, z02_ready, h.blr, z02, zl, zl_ready, a_ready)):
                        dve.wait_ge(ready, now.n + 1)
                        wait(dve, used, now.n)
                        nc.vector.scalar_tensor_tensor(out=dst[:, :], in0=ps_[:, :], scalar=bias[:, :], in1=low[:, :],
                                                       op0=ALU.add, op1=ALU.max).then_inc(done, 1)
                sums(2, g3, a3, min(b3, 2), sq3)
                if now:
                    dve.wait_ge(as_ready, now.n + 1)
                    dve.wait_ge(far_landed[now.slot], 16 * (now.half + 1))
                    wait(dve, us_ready, now.n)
                    nc.vector.scalar_tensor_tensor(out=lself[:, :], in0=far[:, now.slot, :], scalar=FAR, in1=psA[:, :],
                                                   op0=ALU.add, op1=ALU.subtract, reverse1=True
                                                   ).then_inc(lself_ready, 1)
                if last:
                    dve.wait_ge(p_ready, last.n + 1)
                    wait(dve, ptot_ready, last.n)
                    nc.vector.scalar_tensor_tensor(out=pv[:, :], in0=psV[:, :], scalar=h.col("b_l"), in1=p[:, :],
                                                   op0=ALU.add, op1=ALU.mult).then_inc(pv_ready, 1)
                    dve.wait_ge(ps_ready, last.n + 1)
                    wait(dve, num_ready, last.n)
                    nc.vector.scalar_tensor_tensor(out=pvs[:, :], in0=psS[:, :], scalar=h.col("b_l"), in1=ps[:, :],
                                                   op0=ALU.add, op1=ALU.mult).then_inc(pvs_ready, 1)
                if g1:
                    wait(dve, n1n_turned, 2 * g1.n)
                    wait(dve, n1e_turned, g1.n - 1)
                    scaled(0, g1, n1[:, a1:b1, :], pre1[:, a1:b1, :], a1, b1, n1_ready)
                if last:
                    dve.wait_ge(pv_ready, last.n + 1)
                    dve.wait_ge(pvs_ready, last.n + 1)
                    nc.vector.tensor_tensor(pvs[:, :], pvs[:, :], pv[:, :], ALU.add).then_inc(ptot_ready, 1)
                    first = isinstance(last.n, int) and last.n == 0
                    dve.wait_ge(c_ready, last.n + 1)
                    dve.wait_ge(both_ready, last.n + 1)
                    wait(dve, lnd_ready, last.n - 1)
                    nc.vector.tensor_tensor_scan(den[:, s, :], c[:, :], both[:, :],
                                                 0.0 if first else den[:, 1 - s, TILE - 1:TILE],
                                                 ALU.mult, ALU.add).then_inc(den_ready, 1)
                    dve.wait_ge(ptot_ready, last.n + 1)
                    wait(dve, agg_ready, last.n - 1)
                    nc.vector.tensor_tensor_scan(num[:, s, :], c[:, :], pvs[:, :],
                                                 0.0 if first else num[:, 1 - s, TILE - 1:TILE],
                                                 ALU.mult, ALU.add).then_inc(num_ready, 1)
                if g1:
                    wait(dve, sq_ready[1], g1.n)
                    wait(dve, x3_ready, g1.n)
                    for k in range(a1, b1):
                        dve.wait_ge(fe_ready if k == 2 else fn_ready, g1.n if k == 2 else 2 * g1.n + 1 + k)
                        nc.vector.tensor_tensor(pre2[:, k, :], psF[k][:, :], x2r[:, g1.slot, k, :],
                                                ALU.add).then_inc(pre2e_ready if k == 2 else pre2n_ready, 1)
                if last:
                    dve.wait_ge(rden_ready, last.n + 1)
                    dve.wait_ge(num_ready, last.n + 1)
                    wait(dve, ge_ready, last.n)
                    nc.vector.tensor_tensor(agg[:, :], num[:, last.slot, :], rden[:, :], ALU.mult).then_inc(agg_ready, 1)
                if g0:
                    wait(dve, n1_ready, g0.n)
                    for k in range(a0, b0):
                        if k == 2:
                            dve.wait_ge(ee_ready, last.n + 1)
                            dve.wait_ge(x2e_landed[last.slot], 16 * (last.half + 1))
                        else:
                            dve.wait_ge(en_ready, 2 * now.n + 1 + k)
                            dve.wait_ge(x2n_landed[now.slot], 16 * (now.half + 1))
                        nc.vector.tensor_tensor(pre1[:, k, :], psG[k][:, :], x2r[:, g0.slot, k, :],
                                                ALU.add).then_inc(pre1e_ready if k == 2 else pre1n_ready, 1)

            run_steps(dve, 3, step)


def layer3(nc, io, h):
    with ExitStack() as ctx:
        ctx.enter_context(nc.cleanup_on_exit())
        sem = lambda name: nc.alloc_semaphore("f_" + name)
        sb = lambda name, shape, dt=F32: ctx.enter_context(nc.sbuf_tensor("f_" + name, shape, dt))
        bank = lambda name: ctx.enter_context(nc.psum_tensor("f_" + name, [P, TILE], F32))
        table = io["x3"]
        ix = sb("ix", [P, 2, 4], I32)
        to = sb("to", [P, 2, 4], I32)
        xs, x3r = sb("xs", [P, 2, TILE]), sb("x3r", [P, 2, TILE])
        red, reluT = sb("red", [P, 2, TILE]), sb("reluT", [P, TILE])
        pre, sq = sb("pre", [P, 2, TILE]), sb("sq", [P, TILE])
        var, lnv, rstd = sb("var", [P, 4]), sb("lnv", [P, 4]), sb("rstd", [P, 4])
        xo = sb("xo", [P, 2, TILE])
        psT = [bank(f"psT{k}") for k in range(2)]
        psY, psE = bank("psY"), bank("psE")
        src_landed, x3_landed, scattered = [[sem(f"{n}{s}") for s in range(2)] for n in (
            "src_landed", "x3_landed", "scattered")]
        (starts, ix_ready, to_ready, turned, red_ready, y_ready, relu_ready, e_ready, pre_ready, sq_ready, var_ready,
         lnv_ready, rstd_ready, out_ready) = map(sem, (
             "starts", "ix_ready", "to_ready", "turned", "red_ready", "y_ready", "relu_ready", "e_ready", "pre_ready",
             "sq_ready", "var_ready", "lnv_ready", "rstd_ready", "out_ready"))
        block = ctx.enter_context(nc.Block())

        @block.gpsimd
        def _(pool):
            def step(t):
                now, old = t.tile(0), t.tile(2)
                if now:
                    s = now.slot
                    wait(pool, src_landed[s], 64 * now.half)
                    nc.gpsimd.tensor_copy(ix[:, s, :], h.src_row[:, bass.ds(now.n * 4, 4)]).then_inc(ix_ready, 1)
                    wait(pool, turned, now.n - 1)
                    wait_for_dma(pool, ix_ready, now.n + 1, starts)
                    for j in range(4):
                        at = bass.IndirectOffsetOnAxis(ap=ix[:, s, j:j + 1], axis=0)
                        pool.indirect_dma_start(out=quarters(xs[:, s, :])[j], out_offset=None, in_=table,
                                                in_offset=at).then_inc(src_landed[s], 16)
                if old:
                    s = old.slot
                    wait(pool, scattered[s], 64 * old.half)
                    nc.gpsimd.tensor_copy(to[:, s, :], h.end_i[:, bass.ds(old.n * 4, 4)]).then_inc(to_ready, 1)
                    pool.wait_ge(out_ready, old.n + 1)
                    wait_for_dma(pool, to_ready, old.n + 1, starts)
                    for j in range(4):
                        at = bass.IndirectOffsetOnAxis(ap=to[:, s, j:j + 1], axis=0)
                        pool.indirect_dma_start(out=io["out"], out_offset=at, in_=quarters(xo[:, s, :])[j],
                                                in_offset=None, bounds_check=NODE_ROWS - 1,
                                                oob_is_err=False).then_inc(scattered[s], 16)

            run_steps(pool, 2, step)
            for s in range(2):
                pool.wait_ge(scattered[s], 64 * STEPS // 2)

        @block.sync
        def _(sp):
            def step(t):
                now = t.tile(0)
                wait(sp, pre_ready, now.n - 1)
                sp.dma_start(by_row(x3r[:, now.slot, :]), edge_rows(table, now.n)).then_inc(x3_landed[now.slot], 16)

            run_steps(sp, 0, step)

        @block.tensor
        def _(pe):
            def step(t):
                now, last = t.tile(0), t.tile(1)
                if now:
                    s = now.slot
                    pe.wait_ge(src_landed[s], 64 * (now.half + 1))
                    wait(pe, red_ready, now.n - 1)
                    for o, x in zip(quarters(psT[s]), quarters(xs[:, s, :])):
                        ins = nc.tensor.transpose(o, x, h.w["ident"][:, :])
                    ins.then_inc(turned, 1)
                    pe.wait_ge(red_ready, now.n + 1)
                    wait(pe, relu_ready, now.n)
                    nc.tensor.matmul(psY[:, :], h.w["w3t"][:, :], red[:, s, :], start=True, stop=True).then_inc(y_ready, 1)
                    pe.wait_ge(relu_ready, now.n + 1)
                    wait(pe, pre_ready, now.n)
                    for o, x in zip(quarters(psE), quarters(reluT)):
                        ins = nc.tensor.matmul(o, x, h.w["center"][:, :], start=True, stop=True)
                    ins.then_inc(e_ready, 1)

            run_steps(pe, 0, step)

        @block.scalar
        def _(act):
            nc.scalar.preload_act_table_set(LN_EXP)

            def step(t):
                now, last = t.tile(0), t.tile(1)
                if last:
                    act.wait_ge(var_ready, last.n + 1)
                    wait(act, rstd_ready, last.n)
                    nc.scalar.activation(lnv[:, :], var[:, :], ACT.Ln, bias=h.eps[:, :],
                                         scale=1.0 / P).then_inc(lnv_ready, 1)
                    act.wait_ge(lnv_ready, last.n + 1)
                    wait(act, out_ready, last.n)
                    nc.scalar.activation(rstd[:, :], lnv[:, :], ACT.Exp, scale=-0.5).then_inc(rstd_ready, 1)
                if now:
                    act.wait_ge(y_ready, now.n + 1)
                    wait(act, e_ready, now.n)
                    nc.scalar.activation(reluT[:, :], psY[:, :], ACT.Relu).then_inc(relu_ready, 1)
                    act.wait_ge(pre_ready, now.n + 1)
                    wait(act, var_ready, now.n)
                    nc.scalar.activation(sq[:, :], pre[:, now.slot, :], ACT.Square).then_inc(sq_ready, 1)

            run_steps(act, 1, step)

        @block.vector
        def _(dve):
            def step(t):
                now, last = t.tile(0), t.tile(1)
                if last:
                    dve.wait_ge(sq_ready, last.n + 1)
                    wait(dve, rstd_ready, last.n)
                    nc.vector.tensor_reduce(var[:, :], by_row(sq[:, :]), AX_X, ALU.add).then_inc(var_ready, 1)
                if now:
                    s = now.slot
                    dve.wait_ge(turned, now.n + 1)
                    wait(dve, y_ready, now.n - 1)
                    wait(dve, red_ready, now.n)
                    first = 0.0 if isinstance(now.n, int) and now.n == 0 else red[:, 1 - s, TILE - 1:TILE]
                    nc.vector.tensor_tensor_scan(red[:, s, :], h.cont[:, bass.ds(now.n * TILE, TILE)], psT[s][:, :],
                                                 first, ALU.mult, ALU.add).then_inc(red_ready, 1)
                if last:
                    dve.wait_ge(rstd_ready, last.n + 1)
                    wait(dve, scattered[last.slot], 64 * last.half)
                    scale = rstd[:, :].rearrange("p (b o) -> p b o", o=1).to_broadcast([P, 4, P])
                    nc.vector.tensor_tensor(by_row(xo[:, last.slot, :]), by_row(pre[:, last.slot, :]), scale,
                                            ALU.mult).then_inc(out_ready, 1)
                if now:
                    dve.wait_ge(e_ready, now.n + 1)
                    dve.wait_ge(x3_landed[s], 16 * (now.half + 1))
                    wait(dve, out_ready, now.n - 1)
                    nc.vector.scalar_tensor_tensor(out=pre[:, s, :], in0=x3r[:, s, :], scalar=2.0, in1=psE[:, :],
                                                   op0=ALU.mult, op1=ALU.add).then_inc(pre_ready, 1)

            run_steps(dve, 1, step)


def build(nc, io):
    with ExitStack() as ctx:
        sb = lambda name, shape, dt=F32: ctx.enter_context(nc.sbuf_tensor(name, shape, dt))
        h = Held()
        h.w = {name: sb(f"w_{name}", [P, P]) for name in names_of_weights()}
        h.cols = sb("cols", [P, len(names_of_columns())])
        h.col = lambda name: h.cols[:, names_of_columns().index(name):names_of_columns().index(name) + 1]
        square = lambda name: sb(name, [P, P])
        column = lambda name: sb(name, [P, 1])
        per_edge = lambda name: sb(name, [P, COLS], I32)
        h.s1c, h.w_lr, h.att_m = square("s1c"), square("w_lr"), square("att_m")
        h.s_b0, h.s_b1c = square("s_b0"), square("s_b1c")
        h.w_edge_row, h.w_e_row = square("w_edge_row"), square("w_e_row")
        h.avg = square("avg")
        h.b_vs = sb("b_vs", [P, 2])
        h.x01b_node, h.x01b_edge = column("x01b_node"), column("x01b_edge")
        h.blr, h.x2blr, h.bl_out = column("blr"), column("x2blr"), column("bl_out")
        h.b_self, h.x2b_self = column("b_self"), column("x2b_self")
        h.eps, h.eps4, h.den_eps = column("eps"), column("eps4"), column("den_eps")
        h.src_i, h.dst_i, h.end_i = per_edge("src_i"), per_edge("dst_i"), per_edge("end_i")
        h.src_row, h.dst_row = per_edge("src_row"), per_edge("dst_row")
        h.cont = sb("cont", [P, EDGE_ROWS], U8)
        with nc.sbuf_tensor("far", [P, EDGE_ROWS], BF16) as h.far:
            setup(nc, io, h)
            layer0(nc, io, h)
            conv(nc, io, h, 0)
            conv(nc, io, h, 1)
        layer2(nc, io, h)
        layer3(nc, io, h)


def layout(inputs):
    import numpy as np

    a = {k: np.asarray(v) for k, v in inputs.items()}

    def rows_padded(x, n):
        return np.concatenate([x, np.zeros((n - len(x),) + x.shape[1:], x.dtype)])

    def padded(x, fill):
        return np.concatenate([x.reshape(-1), np.full(EDGE_ROWS - EDGES, fill, x.dtype)])

    def columns(x):
        return np.ascontiguousarray(x.reshape(COLS, P).T)

    def chunks(x):
        return x.reshape(2, HALF, P).transpose(1, 0, 2).reshape(HALF, 2 * P)

    src = padded(a["src"], NODES).astype(np.int32)
    dst = padded(a["dst"], NODES).astype(np.int32)
    edge = a["L0_gnn_W_edge"]
    node = a["L0_gnn_W_node"]
    eye = np.eye(P, dtype=np.float32)
    head = np.arange(P)
    out = {
        "x0": rows_padded(a["x"], NODE_ROWS),
        "src": columns(src), "dst": columns(dst),
        "dst_next": columns(np.append(dst[1:], np.int32(-1))),
        "rev": chunks(dst[::-1]), "rev_before": chunks(np.append(np.int32(-1), dst[:0:-1])),
        "flip": np.ascontiguousarray(eye[::-1]),
        "dst_flat": np.insert(dst, 0, np.int32(-1)).reshape(1, -1),
        "ew": padded(a["edge_weight"], 0).reshape(1, -1),
        "ew1": padded(a["edge_weight1"], 0).reshape(1, -1),
        "ew1_cols": columns(padded(a["edge_weight1"], 0)),
        "w_src": edge[0:P], "w_dst": edge[P:2 * P], "w_edge_row": edge[2 * P:],
        "w_node": node[0:P], "w_red": node[P:],
        "w_l": a["L2_gnn_W_l"], "w_r": a["L2_gnn_W_r"], "w_e_row": a["L2_gnn_W_e"],
        "w3t": a["L3_gnn_W"].T,
        "ident": eye, "center": eye - np.float32(1 / P),
        "heads8": np.equal.outer(head // 16, head // 16).astype(np.float32) / 4,
        "blocks4": np.equal.outer(head // 32, head // 32).astype(np.float32),
        "s_row0": a["L1_gnn_s_b0"].reshape(1, P), "s_row1": a["L1_gnn_s_b1"].reshape(1, P),
        "b_edge": a["L0_gnn_b_edge"], "b_node": a["L0_gnn_b_node"],
        "b_l": a["L2_gnn_b_l"], "b_r": a["L2_gnn_b_r"], "w_e": a["L2_gnn_W_e"], "att": a["L2_gnn_att"],
        "g_bias": a["L2_gnn_bias"], "ln_w": a["L2_gnn_ln_w"], "ln_b": a["L2_gnn_ln_b"],
    }
    for k in "qkvs":
        for n in "01":
            out[k + n] = a[f"L1_gnn_{k}_w{n}"]
            out[f"{k}_b{n}"] = a[f"L1_gnn_{k}_b{n}"]
    for name in names_of_columns():
        out[name] = out[name].reshape(P, 1)
    return {k: np.ascontiguousarray(v) for k, v in out.items()}


def program(nc, shapes, kinds=None):
    io = {n: nc.dram_tensor(f"in_{n}", s, t, kind="ExternalInput").ap() for n, (s, t) in shapes.items()}
    for name in ("x1", "h1", "x2", "x3"):
        io[name] = nc.dram_tensor(f"table_{name}", (TABLE_ROWS, P), F32, kind=kinds or "Internal").ap()
    io["far"] = nc.dram_tensor("far_row", (1, EDGE_ROWS), BF16, kind="Internal").ap()
    io["row_of"] = nc.dram_tensor("row_of", (NODE_ROWS, 1), I32, kind=kinds or "Internal").ap()
    io["out"] = nc.dram_tensor("out", (NODE_ROWS, P), F32, kind="ExternalOutput").ap()
    build(nc, io)


def kernel(**inputs):
    import concourse.bacc as bacc
    from concourse.bass_utils import run_bass_kernel_spmd

    nc = bacc.Bacc("TRN2", target_bir_lowering=False, num_devices=1)
    arrays = layout(inputs)
    program(nc, {n: (a.shape, mybir.dt.from_np(a.dtype)) for n, a in arrays.items()})
    r = run_bass_kernel_spmd(nc, [{f"in_{n}": a for n, a in arrays.items()}], core_ids=[0])
    return r.results[0]["out"][:NODES]
```
